# Optimizing a Trainium2 kernel written in Bass

```python
import numpy as np
import jax
import jax.numpy as jnp

def _softmax(x, axis=-1):
    return jax.nn.softmax(x, axis=axis)

def _gelu(x):
    return jax.nn.gelu(x, approximate=True)

def _silu(x):
    return jax.nn.silu(x)

def _sigmoid(x):
    return jax.nn.sigmoid(x)

def _layernorm(x, axis=-1, eps=1e-05):
    m = jnp.mean(x, axis=axis, keepdims=True)
    v = jnp.var(x, axis=axis, keepdims=True)
    return (x - m) / jnp.sqrt(v + eps)

def _scatter_add(tgt, idx, src, axis=0):
    return tgt.at[idx].add(src)

def _segment_sum(src, seg, n):
    return jax.ops.segment_sum(src, seg, n)
kernel_name = 'mk_seq_postln_d1_jaxref_r8_d2a7df'

def setup_inputs(seed: int=0):
    np.random.seed(seed)
    _w = jnp.asarray

    def _L0_attn_setup():
        import jax, jax.numpy as jnp
        import numpy as np
        B, N, DIM = (2, 256, 128)
        H = 16
        HD = DIM // H
        key = jax.random.key(seed)
        ks = jax.random.split(key, 4)
        x = jax.random.normal(ks[0], (B, N, DIM), dtype=jnp.float32)
        w_qkv = jax.random.normal(ks[1], (DIM, 3 * DIM), dtype=jnp.float32) / np.sqrt(DIM)
        w_proj = jax.random.normal(ks[2], (DIM, DIM), dtype=jnp.float32) / np.sqrt(DIM)
        b_proj = jax.random.normal(ks[3], (DIM,), dtype=jnp.float32) * 0.01
        return {'x': x, 'w_qkv': w_qkv, 'w_proj': w_proj, 'b_proj': b_proj}
    _L0_attn_in = _L0_attn_setup()

    def _L0_ffn_setup():
        import jax, jax.numpy as jnp
        import numpy as np
        D_MODEL = 128
        H_SHARED = 256
        H_ROUTED = 128
        N_EXPERTS = 8
        TOP_K = 2
        key = jax.random.key(seed)
        ks = jax.random.split(key, 8)
        B, T = (2, 256)
        sc_d = 1.0 / np.sqrt(D_MODEL)
        sc_hs = 1.0 / np.sqrt(H_SHARED)
        sc_hr = 1.0 / np.sqrt(H_ROUTED)
        return {'x': jax.random.normal(ks[0], (B, T, D_MODEL), dtype=jnp.float32), 'router_w': jax.random.normal(ks[1], (N_EXPERTS, D_MODEL), dtype=jnp.float32) * sc_d, 'router_bias': jnp.zeros((N_EXPERTS,), dtype=jnp.float32), 'sw1': jax.random.normal(ks[2], (D_MODEL, H_SHARED), dtype=jnp.float32) * sc_d, 'sw3': jax.random.normal(ks[3], (D_MODEL, H_SHARED), dtype=jnp.float32) * sc_d, 'sw2': jax.random.normal(ks[4], (H_SHARED, D_MODEL), dtype=jnp.float32) * sc_hs, 'ew1': jax.random.normal(ks[5], (N_EXPERTS, D_MODEL, H_ROUTED), dtype=jnp.float32) * sc_d, 'ew2': jax.random.normal(ks[6], (N_EXPERTS, H_ROUTED, D_MODEL), dtype=jnp.float32) * sc_hr}
    _L0_ffn_in = _L0_ffn_setup()
    _d = {'L0_attn_x': _L0_attn_in['x'], 'L0_attn_w_qkv': _L0_attn_in['w_qkv'], 'L0_attn_w_proj': _L0_attn_in['w_proj'], 'L0_attn_b_proj': _L0_attn_in['b_proj'], 'L0_ffn_router_w': _L0_ffn_in['router_w'], 'L0_ffn_router_bias': _L0_ffn_in['router_bias'], 'L0_ffn_sw1': _L0_ffn_in['sw1'], 'L0_ffn_sw3': _L0_ffn_in['sw3'], 'L0_ffn_sw2': _L0_ffn_in['sw2'], 'L0_ffn_ew1': _L0_ffn_in['ew1'], 'L0_ffn_ew2': _L0_ffn_in['ew2']}
    _x0 = _d['L0_attn_x']
    _d['L0_attn_x'] = jax.random.normal(jax.random.fold_in(jax.random.key(seed), 1), (8, 1024, 128), dtype=_x0.dtype)
    del _x0
    return _d

def reference(L0_attn_x, L0_attn_w_qkv, L0_attn_w_proj, L0_attn_b_proj, L0_ffn_router_w, L0_ffn_router_bias, L0_ffn_sw1, L0_ffn_sw3, L0_ffn_sw2, L0_ffn_ew1, L0_ffn_ew2):

    def _L0_attn_ref(x, w_qkv, w_proj, b_proj):
        import jax, jax.numpy as jnp
        import numpy as np
        B, N, DIM = (2, 256, 128)
        H = 16
        HD = DIM // H
        b, n, c = x.shape
        scale = HD ** (-0.5)
        qkv = jnp.einsum('bnc,cd->bnd', x, w_qkv)
        qkv = qkv.reshape(b, n, 3, H, HD).transpose(2, 0, 3, 1, 4)
        q, k, v = (qkv[0], qkv[1], qkv[2])
        q = q * scale
        attn = jnp.einsum('bhnd,bhmd->bhnm', q, k)
        attn = jax.nn.softmax(attn, axis=-1)
        out = jnp.einsum('bhnm,bhmd->bhnd', attn, v)
        out = out.transpose(0, 2, 1, 3).reshape(b, n, c)
        return jnp.einsum('bnc,cd->bnd', out, w_proj) + b_proj

    def _L0_ffn_ref(x, router_w, router_bias, sw1, sw3, sw2, ew1, ew2):
        import jax, jax.numpy as jnp
        import numpy as np
        D_MODEL = 128
        H_SHARED = 256
        H_ROUTED = 128
        N_EXPERTS = 8
        TOP_K = 2
        B, T, C = x.shape
        xf = x.reshape(-1, C)
        shared_out = jax.nn.silu(xf @ sw1) * (xf @ sw3) @ sw2
        s = jax.nn.sigmoid((xf @ router_w.T).astype(jnp.float32))
        sel_scores = s + router_bias.astype(jnp.float32)
        _, topk_idx = jax.lax.top_k(sel_scores, TOP_K)
        s_sel = jnp.take_along_axis(s, topk_idx, axis=1)
        denom = s_sel.sum(axis=1, keepdims=True)
        gates = jnp.where(denom > 1e-09, s_sel / (denom + 1e-09), 1.0 / TOP_K).astype(x.dtype)
        one_hot = jax.nn.one_hot(topk_idx, N_EXPERTS, dtype=x.dtype)
        comb = jnp.einsum('nke,nk->ne', one_hot, gates)
        h = jax.nn.gelu(jnp.einsum('nd,edh->neh', xf, ew1), approximate=False)
        y = jnp.einsum('neh,ehd->ned', h, ew2)
        routed_out = jnp.einsum('ned,ne->nd', y, comb)
        return (shared_out + routed_out).reshape(B, T, C)
    x = L0_attn_x
    x = _layernorm(x + _L0_attn_ref(x, L0_attn_w_qkv, L0_attn_w_proj, L0_attn_b_proj), axis=-1)
    x = _layernorm(x + _L0_ffn_ref(x, L0_ffn_router_w, L0_ffn_router_bias, L0_ffn_sw1, L0_ffn_sw3, L0_ffn_sw2, L0_ffn_ew1, L0_ffn_ew2), axis=-1)
    return x

_drawn_inputs = setup_inputs


def setup_inputs(seed=0):
    import zlib

    import numpy as np

    out = dict(_drawn_inputs(seed))
    spreads = {'L0_ffn_router_bias': (0.0, 0.1)}
    factors = {}
    for name, (base, spread) in spreads.items():
        noise = np.random.default_rng([zlib.crc32(name.encode()), seed]).standard_normal(out[name].shape)
        drawn = base * np.exp(spread * noise) if base else spread * noise
        out[name] = jnp.asarray(drawn.astype(out[name].dtype))
    for name, factor in factors.items():
        out[name] = (out[name] * factor).astype(out[name].dtype)
    return out
```

```python
from contextlib import ExitStack

import concourse.bass as bass
from concourse import mybir

F32 = mybir.dt.float32
BF16 = mybir.dt.bfloat16
ALU = mybir.AluOpType
ACT = mybir.ActivationFunctionType
AX = mybir.AxisListType

P = 128
PARTS = 6
PAIRS_IN_FLIGHT = 3
EXP_SLOTS = 4
LN_EPS = 1e-5
SAFE = 30.0


def count(it, per, k):
    return it * per + k


def wait(eng, sem, value):
    if isinstance(value, int) and value <= 0:
        return
    eng.wait_ge(sem, value)


def rounds(eng, n, body):
    body(0, True, n == 1)
    if n > 2:
        with eng.Fori(1, n - 1) as it:
            body(it, False, False)
    if n > 1:
        body(n - 1, False, True)


class Chain:

    def __init__(self, eng, sem):
        self.eng, self.sem, self.per, self.lead, self.it, self.k = eng, sem, 0, 0, 0, 0

    def ahead(self):
        self.lead, self.k = self.k, 0

    def begin(self, it, first):
        if not first and not self.per:
            self.per = self.k
        self.it, self.k = it, 0

    def step(self, ins):
        self.k += 1
        ins.then_inc(self.sem, 1)
        self.eng.wait_ge(self.sem, count(self.it, self.per, self.lead + self.k))


def seq_postln_moe_kernel(nc: bass.Bass, xT, x, w_qkv, w_proj, b_proj, router_wT, router_bias,
                          sw1, sw3, sw2, ew1, ew2, out):
    C, T = xT.shape
    N = 1024
    B = T // N
    HEADS = 16
    D = C // HEADS
    E = ew1.shape[0]
    HS = sw1.shape[1]
    SB = HS // P
    NT = N // P
    ROWS = D * PARTS + D
    SHIFT = D * PARTS
    GROUP = 4
    GROUPS = B * HEADS // GROUP
    NC = 512
    CH = N // NC
    scale = float(D) ** -0.5
    ITS = GROUPS // 2
    STEPS = 2 * CH * NT
    CHUNKS = T // NC
    CT = NC // P

    Q_PARTS = (0, 0, 1, 1, 0, 2)
    K_PARTS = (0, 1, 0, 1, 2, 0)

    q_rows = nc.dram_tensor("q_rows", [B * HEADS, ROWS, N], BF16, kind="Internal").ap()
    k_rows = nc.dram_tensor("k_rows", [B * HEADS, SHIFT, N], BF16, kind="Internal").ap()

    with ExitStack() as top:
        def sb(name, shape, dt=F32, ctx=top):
            return ctx.enter_context(nc.sbuf_tensor(name, shape, dt))

        def sem(name, ctx=top):
            return ctx.enter_context(nc.semaphore(name))

        psum = top.enter_context(nc.psum_tensor("psum", [P, 8, NC], F32))
        v_all = sb("v_all", [P, GROUPS // 2, 2, NT, GROUP * D])
        attn_all = sb("attn_all", [P, GROUPS // 2, 2, CH, CT, GROUP * D])
        ident = sb("ident", [P, P])
        loose = sb("loose", [1, 1], mybir.dt.int32)
        v_w = sb("v_w", [P, 2, NT, GROUP, 32])
        q_sb = sb("q_sb", [P, 2, 2, N], BF16)
        k_sb = sb("k_sb", [P, 2, 2, N], BF16)

        with ExitStack() as ctx:
            w_sb = sb("w_sb", [C, 3 * C], ctx=ctx)
            x_sb = sb("x_sb", [C, 2, N], ctx=ctx)
            qk = sb("qk", [C, 2, N], ctx=ctx)
            rest = sb("rest", [C, N], ctx=ctx)
            parts = sb("parts", [C, 2, 2, 3, N], BF16, ctx=ctx)
            minus1 = sb("minus1", [D, 2, N], BF16, ctx=ctx)
            m_ones = sem("m_ones", ctx)
            k_ones = sem("k_ones", ctx)
            STORES = 2 * PARTS + 1
            w_in = sem("w_in", ctx)
            x_in = [sem(f"x_in{i}", ctx) for i in range(2)]
            k_abs = sb("k_abs", [C, 1], ctx=ctx)
            bound = sb("bound", [C, 2, N], BF16, ctx=ctx)
            head_of = sb("head_of", [C, HEADS], BF16, ctx=ctx)
            ones_h = sb("ones_h", [HEADS, 1], ctx=ctx)
            b_max = sb("b_max", [HEADS, B], ctx=ctx)
            b_all = sb("b_all", [HEADS, 1], ctx=ctx)
            above = sb("above", [HEADS, 1], ctx=ctx)
            k_abs_out = sem("k_abs_out", ctx)
            bound_out = sem("bound_out", ctx)
            bound_mm = sem("bound_mm", ctx)
            bound_max = sem("bound_max", ctx)
            b_step = sem("b_step", ctx)
            above_out = sem("above_out", ctx)
            above_mm = sem("above_mm", ctx)
            loose_out = sem("loose_out", ctx)
            h_one = sem("h_one", ctx)
            h_done = sem("h_done", ctx)
            qk_mm = sem("qk_mm", ctx)
            v_mm = sem("v_mm", ctx)
            qk_out = sem("qk_out", ctx)
            v_out = sem("v_out", ctx)
            hi_out = sem("hi_out", ctx)
            split = sem("split", ctx)
            dve_step = sem("dve_step", ctx)
            stored = [sem(f"stored{i}", ctx) for i in range(2)]
            id_one = sem("id_one", ctx)
            id_done = sem("id_done", ctx)
            qk_ps = psum[:, 0:4, :].rearrange("p (s b) n -> p s (b n)", s=2)
            v_ps = psum[:, 4:6, :].rearrange("p b (t n) -> p (b t) n", n=P)
            b_ps = psum[:, 6:8, :].rearrange("p b n -> p (b n)")
            block = ctx.enter_context(nc.Block())

            @block.sync
            def _(sp):
                sp.dma_start(w_sb[:], w_qkv).then_inc(w_in, 16)

                def load_x(it, u):
                    wait(sp, v_mm, count(it, 2, u - 1))
                    sp.dma_start(x_sb[:, u], xT[:, bass.ds((it * 2 + u) * N, N)]).then_inc(x_in[u], 16)

                load_x(0, 0)
                sp.wait_ge(m_ones, 1)
                for hh in range(2):
                    for u in range(2):
                        sp.dma_start(k_sb[64 * hh + SHIFT:64 * hh + ROWS, u], minus1[:]).then_inc(k_ones, 16)

                def body(it, first, last):
                    for u in range(2):
                        if not (last and u == 1):
                            load_x(*((it, 1) if u == 0 else (it + 1, 0)))
                        for s, (rows, order) in enumerate(((q_rows, Q_PARTS), (k_rows, K_PARTS))):
                            sp.wait_ge(split, count(it, 4, 2 * u + s + 1))
                            for t, part in enumerate(order):
                                sp.dma_start(rows[bass.ds((it * 2 + u) * HEADS, HEADS), t * D:(t + 1) * D, :],
                                             parts[:, u, s, part]).then_inc(stored[u], 16)
                        sp.wait_ge(bound_out, count(it, 2, u + 1))
                        sp.dma_start(q_rows[bass.ds((it * 2 + u) * HEADS, HEADS), SHIFT:ROWS, :],
                                     bound[:, u]).then_inc(stored[u], 16)
                rounds(sp, B // 2, body)
                sp.wait_ge(k_ones, 64)
                for u in range(2):
                    sp.wait_ge(stored[u], B // 2 * STORES * 16)

            @block.tensor
            def _(pe):
                pe.wait_ge(w_in, 16)

                def body(it, first, last):
                    for u in range(2):
                        pe.wait_ge(x_in[u], count(it, 16, 16))
                        for s in range(2):
                            wait(pe, qk_out, count(it, 4, 2 * u + s - 1))
                            for c in range(CH):
                                mm = pe.matmul(qk_ps[:, s, c * NC:(c + 1) * NC], w_sb[:, s * C:(s + 1) * C],
                                               x_sb[:, u, c * NC:(c + 1) * NC], start=True, stop=True)
                            mm.then_inc(qk_mm, 1)
                        wait(pe, v_out, count(it, 2, u))
                        for t in range(NT):
                            mm = pe.matmul(v_ps[:, t], x_sb[:, u, t * P:(t + 1) * P], w_sb[:, 2 * C:3 * C],
                                           start=True, stop=True)
                        mm.then_inc(v_mm, 1)
                        if not (first and u == 0):
                            bound_sums(it, u - 1)
                    if last:
                        bound_sums(it, 1)
                pe.wait_ge(h_done, 1)

                def bound_sums(it, u):
                    pe.wait_ge(bound_out, count(it, 2, u + 1))
                    wait(pe, bound_max, count(it, 2, u))
                    for c in range(CH):
                        mm = pe.matmul(b_ps[0:HEADS, c * NC:(c + 1) * NC], head_of[:],
                                       bound[:, u % 2, c * NC:(c + 1) * NC], start=True, stop=True)
                    mm.then_inc(bound_mm, 1)

                rounds(pe, B // 2, body)
                pe.wait_ge(above_out, 1)
                pe.matmul(b_ps[0:1, 0:1], ones_h[:], above[:], start=True, stop=True).then_inc(above_mm, 1)

            @block.scalar
            def _(act):
                def body(it, first, last):
                    for u in range(2):
                        for s in range(2):
                            act.wait_ge(qk_mm, count(it, 4, 2 * u + s + 1))
                            wait(act, bound_out, count(it, 2, u))
                            act.activation(qk[:, s], qk_ps[:, s], ACT.Copy,
                                           scale=scale if s == 0 else 1.0).then_inc(qk_out, 1)
                            act.wait_ge(qk_out, count(it, 4, 2 * u + s + 1))
                            if not first:
                                act.wait_ge(stored[u], count(it, STORES * 16, 0))
                            act.activation(parts[:, u, s, 0], qk[:, s], ACT.Copy).then_inc(hi_out, 1)
                        act.wait_ge(k_abs_out, count(it, 2, u + 1))
                        if not first:
                            act.wait_ge(stored[u], count(it, STORES * 16, 0))
                        act.activation(bound[:, u], qk[:, 0], ACT.Abs, scale=k_abs[:]).then_inc(bound_out, 1)
                        act.wait_ge(v_mm, count(it, 2, u + 1))
                        for r in range(2):
                            for h in range(2):
                                ins = act.activation(v_all[:, bass.ds(4 * it + 2 * u + r, 1), h].rearrange(
                                                         "p o t c -> p (o t) c"),
                                                     v_ps[:, :, (2 * r + h) * GROUP * D:(2 * r + h + 1) * GROUP * D],
                                                     ACT.Copy)
                        ins.then_inc(v_out, 1)
                rounds(act, B // 2, body)

            @block.vector
            def _(dve):
                chain = Chain(dve, dve_step)

                def body(it, first, last):
                    chain.begin(it, first)
                    for u in range(2):
                        for s in range(2):
                            hi, mid, lo = (parts[:, u, s, i] for i in range(3))
                            dve.wait_ge(hi_out, count(it, 4, 2 * u + s + 1))
                            chain.step(dve.tensor_tensor(rest[:], qk[:, s], hi, ALU.subtract))
                            chain.step(dve.tensor_copy(mid, rest[:]))
                            dve.tensor_tensor(lo, rest[:], mid, ALU.subtract).then_inc(split, 1)
                            dve.wait_ge(split, count(it, 4, 2 * u + s + 1))
                        dve.tensor_reduce(k_abs[:], qk[:, 1], AX.X, ALU.max,
                                          apply_absolute_value=True).then_inc(k_abs_out, 1)
                        if not (first and u == 0):
                            largest(it, u - 1)
                    if last:
                        largest(it, 1)

                def largest(it, u):
                    dve.wait_ge(bound_mm, count(it, 2, u + 1))
                    dve.tensor_reduce(b_max[:, bass.ds(it * 2 + u, 1)], b_ps[0:HEADS], AX.X,
                                      ALU.max).then_inc(bound_max, 1)

                rounds(dve, B // 2, body)
                dve.wait_ge(bound_max, B)
                dve.tensor_reduce(b_all[:], b_max[:], AX.X, ALU.max).then_inc(b_step, 1)
                dve.wait_ge(b_step, 1)
                dve.tensor_scalar(above[:], b_all[:], SAFE, None, ALU.is_gt).then_inc(above_out, 1)
                dve.wait_ge(above_mm, 1)
                dve.tensor_copy(loose[:], b_ps[0:1, 0:1]).then_inc(loose_out, 1)

            @block.gpsimd
            def _(pool):
                pool.memset(ident[:], 1.0).then_inc(id_one, 1)
                pool.wait_ge(id_one, 1)
                pool.affine_select(out=ident[:], in_=ident[:], compare_op=ALU.is_equal, fill=0.0, base=0,
                                   pattern=[[-1, P]], channel_multiplier=1).then_inc(id_done, 1)

                pool.memset(minus1[:], -1.0).then_inc(m_ones, 1)
                pool.memset(ones_h[:], 1.0).then_inc(h_one, 1)
                pool.memset(head_of[:], 1.0).then_inc(h_one, 1)
                pool.wait_ge(h_one, 2)
                pool.affine_select(out=head_of[:], in_=head_of[:], compare_op=ALU.is_ge, fill=0.0, base=0,
                                   pattern=[[-D, HEADS]], channel_multiplier=1).then_inc(h_one, 1)
                pool.wait_ge(h_one, 3)
                pool.affine_select(out=head_of[:], in_=head_of[:], compare_op=ALU.is_gt, fill=0.0, base=D,
                                   pattern=[[D, HEADS]], channel_multiplier=-1).then_inc(h_done, 1)

        def load_rows(eng, rows, n, dst, u, it, done):
            for hh in range(2):
                eng.dma_start(dst[64 * hh:64 * hh + n, u],
                              rows[bass.ds((it * 2 + u) * GROUP, GROUP), 0:n, :].rearrange(
                                  "(pair hh) r n -> hh r pair n", hh=2)[hh]).then_inc(done, 16)

        with ExitStack() as ctx:
            mx = sb("mx", [P, 2, NT, GROUP], ctx=ctx)
            mxT = sb("mxT", [GROUP, 2, N], ctx=ctx)
            shift = sb("shift", [GROUP, D, N], BF16, ctx=ctx)
            qk_in = [sem(f"mqk_in{i}", ctx) for i in range(2)]
            s_mm = sem("ms_mm", ctx)
            s_max = sem("ms_max", ctx)
            m_tr = sem("m_tr", ctx)
            m_split = sem("m_split", ctx)
            m_zero = sem("m_zero", ctx)
            m_step = sem("m_step", ctx)
            m_store = sem("m_store", ctx)
            TILES = GROUP * NT
            s_ps = psum[:, 0:4, :].rearrange("p (s b) n -> p s (b n)", s=2)
            t_ps = psum[:, 4:6, :].rearrange("p b n -> p (b n)")
            block = ctx.enter_context(nc.Block())

            @block.sync
            def _(sp):
                def body(it, first, last):
                    for u in range(2):
                        wait(sp, s_mm, count(it, 2 * TILES, (u - 1) * TILES))
                        load_rows(sp, q_rows, SHIFT, q_sb, u, it, qk_in[u])
                        load_rows(sp, k_rows, SHIFT, k_sb, u, it, qk_in[u])
                with sp.If(sp.value_load(loose[:], min_val=0, max_val=HEADS) > 0):
                    rounds(sp, ITS, body)

            @block.tensor
            def _(pe):
                def body(it, first, last):
                    for u in range(2):
                        pe.wait_ge(qk_in[u], count(it, 64, 64))
                        for i in range(TILES):
                            j, t = divmod(i, NT)
                            pair, hh = divmod(j, 2)
                            rows = slice(64 * hh, 64 * hh + SHIFT)
                            wait(pe, s_max, count(it, 2 * TILES, u * TILES + i - 1))
                            for c in range(CH):
                                mm = pe.matmul(s_ps[:, i % 2, c * NC:(c + 1) * NC],
                                               q_sb[rows, u, pair, t * P:(t + 1) * P],
                                               k_sb[rows, u, pair, c * NC:(c + 1) * NC], start=True, stop=True)
                            mm.then_inc(s_mm, 1)
                        pe.wait_ge(s_max, count(it, 2 * TILES, (u + 1) * TILES))
                        wait(pe, m_split, count(it, 2, u))
                        for t in range(NT):
                            mm = pe.transpose(t_ps[0:GROUP, t * P:(t + 1) * P], mx[:, u, t, :], ident[:])
                        mm.then_inc(m_tr, 1)
                with pe.If(pe.value_load(loose[:], min_val=0, max_val=HEADS) > 0):
                    rounds(pe, ITS, body)

            @block.vector
            def _(dve):
                chain = Chain(dve, m_step)

                def body(it, first, last):
                    chain.begin(it, first)
                    for u in range(2):
                        for i in range(TILES):
                            j, t = divmod(i, NT)
                            dve.wait_ge(s_mm, count(it, 2 * TILES, u * TILES + i + 1))
                            dve.tensor_reduce(mx[:, u, t, j:j + 1], s_ps[:, i % 2], AX.X,
                                              ALU.max).then_inc(s_max, 1)
                        dve.wait_ge(m_tr, count(it, 2, u + 1))
                        wait(dve, m_store, count(it, 32, 16 * u))
                        chain.step(dve.tensor_copy(shift[:, 0], t_ps[0:GROUP]))
                        chain.step(dve.tensor_tensor(mxT[:, 0], t_ps[0:GROUP], shift[:, 0], ALU.subtract))
                        chain.step(dve.tensor_copy(shift[:, 1], mxT[:, 0]))
                        chain.step(dve.tensor_tensor(mxT[:, 1], mxT[:, 0], shift[:, 1], ALU.subtract))
                        dve.tensor_copy(shift[:, 2], mxT[:, 1]).then_inc(m_split, 1)
                with dve.If(dve.value_load(loose[:], min_val=0, max_val=HEADS) > 0):
                    dve.memset(shift[:], 0.0).then_inc(m_zero, 1)
                    dve.wait_ge(m_zero, 1)
                    rounds(dve, ITS, body)

            @block.gpsimd
            def _(pool):
                def body(it, first, last):
                    for u in range(2):
                        pool.wait_ge(m_split, count(it, 2, u + 1))
                        pool.dma_start(q_rows[bass.ds((it * 2 + u) * GROUP, GROUP), SHIFT:ROWS, :],
                                       shift[:]).then_inc(m_store, 16)
                with pool.If(pool.value_load(loose[:], min_val=0, max_val=HEADS) > 0):
                    rounds(pool, ITS, body)
                    pool.wait_ge(m_store, GROUPS * 16)

        with ExitStack() as ctx:
            p_sb = sb("p_sb", [P, EXP_SLOTS, GROUP, NC], ctx=ctx)
            o_sb = sb("o_sb", [P, 2, NC], ctx=ctx)
            r_sb = sb("r_sb", [P, CT, GROUP], ctx=ctx)
            rows_in = [sem(f"rows_in{i}", ctx) for i in range(2)]
            v_ready = sem("v_ready", ctx)
            v_zero = sem("v_zero", ctx)
            scores = sem("scores", ctx)
            exps = sem("exps", ctx)
            pv = sem("pv", ctx)
            o_mm = sem("o_mm", ctx)
            o_out = sem("o_out", ctx)
            o_tr = sem("o_tr", ctx)
            recip = sem("recip", ctx)
            o_norm = sem("o_norm", ctx)
            block = ctx.enter_context(nc.Block())
            PAIRS = 2 * STEPS
            OCH = 2 * CH

            def slot(p):
                return p % PAIRS % PAIRS_IN_FLIGHT

            def last_user(p):
                return max(r for r in range(p - 2 * PAIRS_IN_FLIGHT, p) if slot(r) == slot(p))

            @block.sync
            def _(sp):
                def body(it, first, last):
                    for u in range(2):
                        wait(sp, scores, count(it, PAIRS, (u + 1) * PAIRS // 2 - PAIRS))
                        load_rows(sp, q_rows, ROWS, q_sb, u, it, rows_in[u])
                        load_rows(sp, k_rows, SHIFT, k_sb, u, it, rows_in[u])
                rounds(sp, ITS, body)

            @block.gpsimd
            def _(pool):
                pool.memset(v_w[:], 0.0).then_inc(v_zero, 1)
                pool.wait_ge(v_zero, 1)
                pool.memset(v_w[:, :, :, :, D:D + 1], 1.0).then_inc(v_zero, 1)

                def body(it, first, last):
                    for u in range(2):
                        wait(pool, pv, count(it, STEPS, (u + 1) * STEPS // 2 - STEPS))
                        src = v_all[:, bass.ds(it, 1), u].rearrange("p o t (j d) -> p (o t) j d", j=GROUP)
                        pool.tensor_copy(v_w[:, u, :, :, 0:D], src).then_inc(v_ready, 1)
                rounds(pool, ITS, body)

            @block.tensor
            def _(pe):
                pe.wait_ge(v_zero, 2)

                def score_pair(it, p):
                    nxt, q = divmod(p, PAIRS)
                    u, q = divmod(q, CH * NT * 2)
                    c, q = divmod(q, NT * 2)
                    t, pair = divmod(q, 2)
                    if c == 0 and t == 0 and pair == 0:
                        pe.wait_ge(rows_in[u], count(it + nxt, 64, 64))
                    wait(pe, exps, count(it, PAIRS, last_user(p) + 1))
                    for hh in range(2):
                        rows = slice(64 * hh, 64 * hh + ROWS)
                        mm = pe.matmul(psum[:, 2 * slot(p) + hh], k_sb[rows, u, pair, t * P:(t + 1) * P],
                                       q_sb[rows, u, pair, c * NC:(c + 1) * NC], start=True, stop=True)
                    mm.then_inc(scores, 1)

                def weigh(it, s):
                    o, t = divmod(s, NT)
                    u = o // CH
                    if o % CH == 0 and t == 0:
                        pe.wait_ge(v_ready, count(it, 2, u + 1))
                    if t == 0:
                        wait(pe, o_norm, count(it, OCH, o - 1))
                    pe.wait_ge(exps, count(it, PAIRS, 2 * s + 2))
                    for j in range(GROUP):
                        mm = pe.matmul(psum[32 * j:32 * j + 32, 6 + o % 2], v_w[:, u, t, j, :],
                                       p_sb[:, s % EXP_SLOTS, j, :], start=(t == 0), stop=(t == NT - 1))
                    mm.then_inc(pv, 1)

                def turn(it, o):
                    pe.wait_ge(o_out, count(it, OCH, o + 1))
                    for t in range(CT):
                        mm = pe.transpose(psum[:, 6 + o % 2, t * P:(t + 1) * P], o_sb[:, o % 2, t * P:(t + 1) * P],
                                          ident[:])
                    mm.then_inc(o_tr, 1)

                for p in range(PAIRS_IN_FLIGHT):
                    score_pair(0, p)

                def body(it, first, last):
                    for s in range(STEPS):
                        for p in (2 * s + PAIRS_IN_FLIGHT, 2 * s + PAIRS_IN_FLIGHT + 1):
                            if not (last and p >= PAIRS):
                                score_pair(it, p)
                        weigh(it, s)
                        if s % NT == 1 and not (first and s < NT):
                            turn(it, s // NT - 1)
                    if last:
                        turn(it, OCH - 1)
                rounds(pe, ITS, body)

            @block.scalar
            def _(act):
                def body(it, first, last):
                    for p in range(PAIRS):
                        s, pair = divmod(p, 2)
                        act.wait_ge(scores, count(it, PAIRS, p + 1))
                        if pair == 0:
                            wait(act, pv, count(it, STEPS, s - EXP_SLOTS + 1))
                        act.activation(p_sb[:, s % EXP_SLOTS, 2 * pair:2 * pair + 2, :],
                                       psum[:, 2 * slot(p):2 * slot(p) + 2, :], ACT.Exp).then_inc(exps, 1)
                rounds(act, ITS, body)

            @block.vector
            def _(dve):
                def body(it, first, last):
                    for o in range(OCH):
                        dve.wait_ge(pv, count(it, STEPS, NT * (o + 1)))
                        dve.tensor_copy(o_sb[:, o % 2], psum[:, 6 + o % 2]).then_inc(o_out, 1)
                        dve.wait_ge(o_tr, count(it, OCH, o + 1))
                        turned = psum[:, 6 + o % 2, :].rearrange("p (t j r) -> p t j r", t=CT, j=GROUP)
                        dve.reciprocal(r_sb[:], turned[:, :, :, D]).then_inc(recip, 1)
                        dve.wait_ge(recip, count(it, OCH, o + 1))
                        dst = attn_all[:, bass.ds(it, 1), o // CH, o % CH].rearrange(
                            "p o t (j d) -> p (o t) j d", j=GROUP)
                        dve.tensor_tensor(dst, turned[:, :, :, 0:D],
                                          r_sb[:].unsqueeze(3).broadcast_to([P, CT, GROUP, D]),
                                          ALU.mult).then_inc(o_norm, 1)
                rounds(dve, ITS, body)

        mixed_tail(nc, top, psum, attn_all, ident, x, w_proj, b_proj, router_wT, router_bias,
                   sw1, sw3, sw2, ew1, ew2, out)


def mixed_tail(nc, top, psum, attn_all, ident, x, w_proj, b_proj, router_wT, router_bias,
               sw1, sw3, sw2, ew1, ew2, out):
    T, C = x.shape
    E, _, H = ew1.shape
    SB = sw1.shape[1] // P
    NC = 512
    CT = NC // P
    CHUNKS = T // NC
    CH = 2
    QUARTERS = attn_all.shape[1] * 2 * CH // CHUNKS
    UPS = 2 * SB + E
    DOWNS = 1 + E
    H_BANKS = (2, 3, 4)
    Y_BANKS = (5, 6, 7)

    with ExitStack() as ctx:
        def sb(name, shape, dt=F32):
            return ctx.enter_context(nc.sbuf_tensor(name, shape, dt))

        def sem(name):
            return ctx.enter_context(nc.semaphore(name))

        wp = sb("wp", [C, C])
        rw = sb("rw", [C, E])
        s1 = sb("s1", [C, SB * P])
        s3 = sb("s3", [C, SB * P])
        s2 = sb("s2", [P, SB, C])
        e1 = sb("e1", [C, E, H])
        e2 = sb("e2", [H, E, C])
        pbias = sb("pbias", [P, C])
        rbias = sb("rbias", [P, E])
        before = sb("before", [P, E, E])
        x_t = sb("x_t", [P, 2, CT, C])
        a_t = sb("a_t", [P, 2, CT, C])
        aT = sb("aT", [C, NC])
        u1 = sb("u1", [P, CT, C])
        x1 = sb("x1", [P, 2, CT, C])
        x1T = sb("x1T", [C, 2, NC])
        st = sb("st", [P, CT, 6])
        mean = sb("mean", [P, CT])
        apart = sb("apart", [P, CT])
        ve = sb("ve", [P, CT])
        rstd = sb("rstd", [P, CT])
        neg_half = sb("neg_half", [P, CT])
        sg = sb("sg", [P, 2, CT, E])
        sel = sb("sel", [P, CT, E])
        gt = sb("gt", [P, CT, E, E])
        eq = sb("eq", [P, CT, E, E])
        mask = sb("mask", [P, CT, E])
        sm = sb("sm", [P, CT, E])
        hm = sb("hm", [P, CT, E])
        den = sb("den", [P, CT])
        den1 = sb("den1", [P, CT])
        okd = sb("okd", [P, CT])
        rden = sb("rden", [P, CT])
        half = sb("half", [P, CT])
        comb = sb("comb", [P, CT, E])
        sig = sb("sig", [P, 2, NC])
        silu = sb("silu", [P, 2, NC])
        gated = sb("gated", [P, SB, NC])
        act_h = sb("act_h", [H, 3, NC])
        acc = sb("acc", [P, CT, C])
        o_t = sb("o_t", [P, 2, CT, C])

        w_in = sem("tw_in")
        consts = sem("consts")
        x_in = [sem(f"tx_in{i}") for i in range(2)]
        x_biased = sem("x_biased")
        a_ready = sem("a_ready")
        a_tr = sem("a_tr")
        a_out = sem("a_out")
        proj = sem("proj")
        u_ready = sem("u_ready")
        var_in = [sem(f"var_in{i}") for i in range(2)]
        std_out = [sem(f"std_out{i}") for i in range(2)]
        x1_ready = sem("x1_ready")
        x1_tr = sem("x1_tr")
        x1T_out = sem("x1T_out")
        logits = sem("logits")
        sig_out = sem("sig_out")
        comb_out = sem("comb_out")
        up = sem("up")
        sig_h = sem("sig_h")
        silu_out = sem("silu_out")
        gated_out = sem("gated_out")
        gelu_out = sem("gelu_out")
        down = sem("down")
        added = sem("added")
        dve_step = sem("t_step")
        pool_step = sem("p_step")
        normed = sem("normed")
        stored = [sem(f"t_stored{i}") for i in range(2)]
        WEIGHTS = 9

        block = ctx.enter_context(nc.Block())
        ROUNDS = CHUNKS // CH

        def banks(i):
            return psum[:, i].rearrange("p (t c) -> p t c", t=CT)

        @block.sync
        def _(sp):
            def load_x(it, u):
                wait(sp, u_ready, count(it, CH, u - 1))
                sp.dma_start(x_t[:, u], x[bass.ds((it * CH + u) * NC, NC), :].rearrange(
                    "(t p) c -> p t c", p=P)).then_inc(x_in[u], 16)

            for dst, src in ((wp, w_proj), (rw, router_wT), (s1, sw1), (s3, sw3),
                             (s2, sw2.rearrange("(s h) c -> h s c", h=P)),
                             (e1, ew1.rearrange("e c h -> c e h")), (e2, ew2.rearrange("e h c -> h e c")),
                             (pbias, b_proj), (rbias, router_bias)):
                sp.dma_start(dst[:], src).then_inc(w_in, 16)

            def body(it, first, last):
                for u in range(CH):
                    load_x(it, u)
                    if not (first and u == 0):
                        v = (u - 1) % CH
                        done = it * CH + u - 1
                        sp.wait_ge(normed, count(it, CH, u))
                        sp.dma_start(out[bass.ds(done * NC, NC), :].rearrange("(t p) c -> p t c", p=P),
                                     o_t[:, v]).then_inc(stored[v], 16)
            rounds(sp, ROUNDS, body)
            sp.wait_ge(normed, CHUNKS)
            sp.dma_start(out[(CHUNKS - 1) * NC:, :].rearrange("(t p) c -> p t c", p=P),
                         o_t[:, CH - 1]).then_inc(stored[CH - 1], 16)
            for v in range(CH):
                sp.wait_ge(stored[v], ROUNDS * 16)

        @block.gpsimd
        def _(pool):
            pool.memset(neg_half[:], -0.5).then_inc(consts, 1)
            pool.memset(before[:], 1.0).then_inc(consts, 1)
            pool.wait_ge(consts, 2)
            pool.affine_select(out=before[:], in_=before[:], compare_op=ALU.is_gt, fill=0.0, base=0,
                               pattern=[[1, E], [-1, E]], channel_multiplier=0).then_inc(consts, 1)
            pool.wait_ge(w_in, 16 * WEIGHTS)
            pool.wait_ge(consts, 3)

            def front(it, u):
                wait(pool, a_tr, count(it, CH, u - 1))
                for g in range(QUARTERS):
                    src = attn_all[:, bass.ds(it * 2 + g // 2, 1), g % 2, u].rearrange("p o t c -> p (o t) c")
                    ins = pool.tensor_copy(a_t[:, u, :, g * (C // QUARTERS):(g + 1) * (C // QUARTERS)], src)
                ins.then_inc(a_ready, 1)
                pool.wait_ge(x_in[u], count(it, 16, 16))
                pool.tensor_tensor(x_t[:, u], x_t[:, u], pbias[:].unsqueeze(1).broadcast_to([P, CT, C]),
                                   ALU.add).then_inc(x_biased, 1)
                power(it, u, 0)

            def power(it, u, which):
                pool.wait_ge(var_in[which], count(it, CH, u + 1))
                pool.tensor_tensor(rstd[:], ve[:], neg_half[:], ALU.pow).then_inc(std_out[which], 1)

            front(0, 0)

            def body(it, first, last):
                for u in range(CH):
                    if not (last and u == CH - 1):
                        front(*((it, u + 1) if u + 1 < CH else (it + 1, 0)))
                    power(it, u, 1)
            rounds(pool, ROUNDS, body)

        @block.tensor
        def _(pe):
            pe.wait_ge(w_in, 16 * WEIGHTS)

            def front_attn(it, u):
                pe.wait_ge(a_ready, count(it, CH, u + 1))
                wait(pe, x1T_out, count(it, CH, u))
                for t in range(CT):
                    mm = pe.transpose(psum[:, 0, t * P:(t + 1) * P], a_t[:, u, t, :], ident[:])
                mm.then_inc(a_tr, 1)

            def front_proj(it, u):
                pe.wait_ge(a_out, count(it, CH, u + 1))
                wait(pe, sig_out, count(it, CH, u))
                for t in range(CT):
                    mm = pe.matmul(psum[:, 1, t * P:(t + 1) * P], aT[:, t * P:(t + 1) * P], wp[:],
                                   start=True, stop=True)
                mm.then_inc(proj, 1)

            def front_turn(it, u):
                pe.wait_ge(x1_ready, count(it, CH, u + 1))
                for t in range(CT):
                    mm = pe.transpose(psum[:, 0, t * P:(t + 1) * P], x1[:, u, t, :], ident[:])
                mm.then_inc(x1_tr, 1)

            def front_router(it, u):
                pe.wait_ge(x1T_out, count(it, CH, u + 1))
                for t in range(CT):
                    mm = pe.matmul(psum[:, 1, t * E:(t + 1) * E], x1T[:, u, t * P:(t + 1) * P], rw[:],
                                   start=True, stop=True)
                mm.then_inc(logits, 1)

            def rise(it, u, n, weights):
                wait(pe, *up_free(it, u, n - 3))
                pe.matmul(psum[:, H_BANKS[n % 3]], weights, x1T[:, u], start=True, stop=True).then_inc(up, 1)

            def up_free(it, u, n):
                if n < 0:
                    u, n = u - 1, n + UPS
                if n < 2 * SB:
                    return gated_out if n % 2 else silu_out, count(it, CH * SB, SB * u + n // 2 + 1)
                return gelu_out, count(it, CH * E, E * u + n - 2 * SB + 1)

            def fall(it, u, n):
                wait(pe, added, count(it, CH * DOWNS, DOWNS * u + n - 2))
                if n == 0:
                    pe.wait_ge(gated_out, count(it, CH * SB, SB * (u + 1)))
                else:
                    pe.wait_ge(gelu_out, count(it, CH * E, E * u + n))
                y = banks(Y_BANKS[n % 3])
                for t in range(CT):
                    tok = slice(t * P, (t + 1) * P)
                    if n:
                        mm = pe.matmul(y[:, t], act_h[:, (n - 1) % 3, tok], e2[:, n - 1], start=True, stop=True)
                    else:
                        for s in range(SB):
                            mm = pe.matmul(y[:, t], gated[:, s, tok], s2[:, s], start=(s == 0), stop=(s == SB - 1))
                mm.then_inc(down, 1)

            for stage in (front_attn, front_proj, front_turn, front_router):
                stage(0, 0)

            def body(it, first, last):
                for u in range(CH):
                    ahead = (it, u + 1) if u + 1 < CH else (it + 1, 0)
                    front = [] if last and u == CH - 1 else [front_attn, front_proj, front_turn, front_router]

                    def next_front():
                        if front:
                            front.pop(0)(*ahead)

                    for s in range(SB):
                        rise(it, u, 2 * s, s1[:, s * P:(s + 1) * P])
                        rise(it, u, 2 * s + 1, s3[:, s * P:(s + 1) * P])
                        if s == 0:
                            next_front()
                    rise(it, u, 2 * SB, e1[:, 0])
                    next_front()
                    rise(it, u, 2 * SB + 1, e1[:, 1])
                    fall(it, u, 0)
                    for e in range(2, E + 2):
                        if e < E:
                            rise(it, u, 2 * SB + e, e1[:, e])
                        fall(it, u, e - 1)
                        if e in (E // 2, E // 2 + 2):
                            next_front()
            rounds(pe, ROUNDS, body)

        @block.scalar
        def _(act):
            def take_attn(it, u):
                act.wait_ge(a_tr, count(it, CH, u + 1))
                wait(act, proj, count(it, CH, u))
                act.activation(aT[:], psum[:, 0], ACT.Copy).then_inc(a_out, 1)

            def take_x1T(it, u):
                act.wait_ge(x1_tr, count(it, CH, u + 1))
                wait(act, up, count(it, CH * UPS, UPS * (u - 1)))
                act.activation(x1T[:, u], psum[:, 0], ACT.Copy).then_inc(x1T_out, 1)

            def route(it, u):
                act.wait_ge(logits, count(it, CH, u + 1))
                wait(act, comb_out, count(it, CH, u - 1))
                act.activation(sg[:, u], psum[:, 1, 0:CT * E].rearrange("p (t e) -> p t e", e=E),
                               ACT.Sigmoid).then_inc(sig_out, 1)

            take_attn(0, 0)
            take_x1T(0, 0)

            def body(it, first, last):
                for u in range(CH):
                    ahead = (it, u + 1) if u + 1 < CH else (it + 1, 0)
                    more = not (last and u == CH - 1)
                    route(it, u)
                    for s in range(SB):
                        act.wait_ge(up, count(it, CH * UPS, UPS * u + 2 * s + 1))
                        wait(act, silu_out, count(it, CH * SB, SB * u + s - 1))
                        act.activation(sig[:, s % 2], psum[:, H_BANKS[2 * s % 3]], ACT.Sigmoid).then_inc(sig_h, 1)
                    for e in range(E):
                        if e == 0 and more:
                            take_attn(*ahead)
                        if e == E // 2 + 1 and more:
                            take_x1T(*ahead)
                        act.wait_ge(up, count(it, CH * UPS, UPS * u + 2 * SB + e + 1))
                        user = e - 3 if e >= 3 else max(range(e, E, 3)) - E - 1
                        wait(act, down, count(it, CH * DOWNS, DOWNS * u + user + 2))
                        act.activation(act_h[:, e % 3], psum[:, H_BANKS[(2 * SB + e) % 3]],
                                       ACT.Gelu).then_inc(gelu_out, 1)
            rounds(act, ROUNDS, body)

        @block.vector
        def _(dve):
            dve.wait_ge(w_in, 16 * WEIGHTS)
            dve.wait_ge(consts, 3)
            chain = Chain(dve, dve_step)

            def norm(it, u, which, src, dst, done):
                for t in range(CT):
                    ins = dve.bn_stats(st[:, t], src[:, t])
                chain.step(ins)
                (mean_e, var_e), (mean_o, var_o) = ((st[:, :, 3 * i + 1], st[:, :, 3 * i + 2]) for i in range(2))
                dve.tensor_tensor(mean[:], mean_e, mean_o, ALU.add)
                dve.tensor_tensor(apart[:], mean_e, mean_o, ALU.subtract)
                chain.step(dve.tensor_tensor(ve[:], var_e, var_o, ALU.add))
                dve.tensor_scalar(mean[:], mean[:], 0.5, None, ALU.mult)
                dve.tensor_scalar(ve[:], ve[:], 1.0 / C, LN_EPS, ALU.mult, ALU.add)
                chain.step(dve.scalar_tensor_tensor(out=apart[:], in0=apart[:], scalar=0.25, in1=apart[:],
                                                    op0=ALU.mult, op1=ALU.mult))
                dve.tensor_tensor(ve[:], ve[:], apart[:], ALU.add).then_inc(var_in[which], 1)
                dve.wait_ge(std_out[which], count(it, CH, u + 1))
                for t in range(CT):
                    ins = dve.tensor_scalar(dst[:, t], src[:, t], mean[:, t:t + 1], rstd[:, t:t + 1],
                                            ALU.subtract, ALU.mult)
                ins.then_inc(done, 1)

            def front_norm(it, u):
                dve.wait_ge(proj, count(it, CH, u + 1))
                dve.wait_ge(x_biased, count(it, CH, u + 1))
                dve.tensor_tensor(u1[:], banks(1), x_t[:, u], ALU.add).then_inc(u_ready, 1)
                dve.wait_ge(u_ready, count(it, CH, u + 1))
                norm(it, u, 0, u1, x1[:, u], x1_ready)

            def gates(it, u):
                s = sg[:, u]
                dve.wait_ge(sig_out, count(it, CH, u + 1))
                chain.step(dve.tensor_tensor(sel[:], s, rbias[:].unsqueeze(1).broadcast_to([P, CT, E]), ALU.add))
                one = sel[:].unsqueeze(3).broadcast_to([P, CT, E, E])
                other = sel[:].unsqueeze(2).broadcast_to([P, CT, E, E])
                dve.tensor_tensor(gt[:], other, one, ALU.is_gt)
                chain.step(dve.tensor_tensor(eq[:], other, one, ALU.is_equal))
                chain.step(dve.tensor_tensor(eq[:], eq[:], before[:].unsqueeze(1).broadcast_to([P, CT, E, E]),
                                             ALU.mult))
                chain.step(dve.tensor_tensor(gt[:], gt[:], eq[:], ALU.add))
                chain.step(dve.tensor_reduce(mask[:], gt[:], AX.X, ALU.add))
                chain.step(dve.tensor_scalar(mask[:], mask[:], 1.5, None, ALU.is_lt))
                chain.step(dve.tensor_tensor(sm[:], mask[:], s, ALU.mult))
                chain.step(dve.tensor_reduce(den[:], sm[:], AX.X, ALU.add))
                dve.tensor_scalar(okd[:], den[:], 1e-9, None, ALU.is_gt)
                chain.step(dve.tensor_scalar(den1[:], den[:], 1e-9, None, ALU.add))
                dve.tensor_scalar(half[:], okd[:], -0.5, 0.5, ALU.mult, ALU.add)
                chain.step(dve.reciprocal(rden[:], den1[:]))
                dve.tensor_tensor(hm[:], mask[:], half[:].unsqueeze(2).broadcast_to([P, CT, E]), ALU.mult)
                chain.step(dve.tensor_tensor(rden[:], rden[:], okd[:], ALU.mult))
                chain.step(dve.tensor_tensor(sm[:], sm[:], rden[:].unsqueeze(2).broadcast_to([P, CT, E]), ALU.mult))
                dve.tensor_tensor(comb[:], sm[:], hm[:], ALU.add).then_inc(comb_out, 1)
                dve.wait_ge(comb_out, count(it, CH, u + 1))

            def add_expert(it, u, n):
                dve.wait_ge(down, count(it, CH * DOWNS, DOWNS * u + n + 1))
                y = banks(Y_BANKS[n % 3])
                if n == 0:
                    dve.tensor_tensor(acc[:], y, x1[:, u], ALU.add).then_inc(added, 1)
                else:
                    for t in range(CT):
                        ins = dve.scalar_tensor_tensor(out=acc[:, t], in0=y[:, t], scalar=comb[:, t, n - 1:n],
                                                       in1=acc[:, t], op0=ALU.mult, op1=ALU.add)
                    ins.then_inc(added, 1)
                dve.wait_ge(added, count(it, CH * DOWNS, DOWNS * u + n + 1))

            front_norm(0, 0)
            chain.ahead()

            def body(it, first, last):
                chain.begin(it, first)
                for u in range(CH):
                    ahead = (it, u + 1) if u + 1 < CH else (it + 1, 0)
                    more = not (last and u == CH - 1)
                    for s in range(SB):
                        dve.wait_ge(sig_h, count(it, CH * SB, SB * u + s + 1))
                        dve.tensor_tensor(silu[:, s % 2], psum[:, H_BANKS[2 * s % 3]], sig[:, s % 2],
                                          ALU.mult).then_inc(silu_out, 1)
                        dve.wait_ge(silu_out, count(it, CH * SB, SB * u + s + 1))
                        dve.wait_ge(up, count(it, CH * UPS, UPS * u + 2 * s + 2))
                        wait(dve, down, count(it, CH * DOWNS, DOWNS * (u - 1) + 1))
                        dve.tensor_tensor(gated[:, s], psum[:, H_BANKS[(2 * s + 1) % 3]], silu[:, s % 2],
                                          ALU.mult).then_inc(gated_out, 1)
                    gates(it, u)
                    add_expert(it, u, 0)
                    if more:
                        front_norm(*ahead)
                    for n in range(1, DOWNS):
                        add_expert(it, u, n)
                    if not first:
                        dve.wait_ge(stored[u], count(it, 16, 0))
                    norm(it, u, 1, acc, o_t[:, u], normed)
            rounds(dve, ROUNDS, body)


def kernel(L0_attn_x, L0_attn_w_qkv, L0_attn_w_proj, L0_attn_b_proj, L0_ffn_router_w, L0_ffn_router_bias,
           L0_ffn_sw1, L0_ffn_sw3, L0_ffn_sw2, L0_ffn_ew1, L0_ffn_ew2):
    import numpy as np
    import concourse.bacc as bacc
    from concourse.bass_utils import run_bass_kernel_spmd

    x = np.asarray(L0_attn_x)
    b, n, c = x.shape
    x = np.ascontiguousarray(x.reshape(b * n, c))
    rows = np.zeros((P, 1), np.float32).shape[0]
    arrays = {
        "xT": np.ascontiguousarray(x.T), "x": x, "w_qkv": np.asarray(L0_attn_w_qkv),
        "w_proj": np.asarray(L0_attn_w_proj),
        "b_proj": np.ascontiguousarray(np.broadcast_to(np.asarray(L0_attn_b_proj), (rows, c))),
        "router_wT": np.ascontiguousarray(np.asarray(L0_ffn_router_w).T),
        "router_bias": np.ascontiguousarray(
            np.broadcast_to(np.asarray(L0_ffn_router_bias), (rows, L0_ffn_router_bias.shape[0]))),
        "sw1": np.asarray(L0_ffn_sw1), "sw3": np.asarray(L0_ffn_sw3), "sw2": np.asarray(L0_ffn_sw2),
        "ew1": np.asarray(L0_ffn_ew1), "ew2": np.asarray(L0_ffn_ew2),
    }
    nc = bacc.Bacc("TRN2", target_bir_lowering=False, num_devices=1)
    args = [nc.dram_tensor(f"in_{k}", a.shape, mybir.dt.from_np(a.dtype), kind="ExternalInput").ap()
            for k, a in arrays.items()]
    out = nc.dram_tensor("result", x.shape, F32, kind="ExternalOutput").ap()
    seq_postln_moe_kernel(nc, *args, out)
    r = run_bass_kernel_spmd(nc, [{f"in_{k}": a for k, a in arrays.items()}], core_ids=[0])
    return r.results[0]["result"].reshape(b, n, c)
```

```python
from contextlib import ExitStack

import concourse.bass as bass
from concourse import mybir

F32 = mybir.dt.float32
BF16 = mybir.dt.bfloat16
ALU = mybir.AluOpType
ACT = mybir.ActivationFunctionType
AX = mybir.AxisListType

P = 128
PARTS = 6
PAIRS_IN_FLIGHT = 3
EXP_SLOTS = 4
WARM_UP = 5
TAIL_WARM_UP = 3
LN_EPS = 1e-5
SAFE = 30.0


def count(it, per, k):
    return it * per + k


def wait(eng, sem, value):
    if isinstance(value, int) and value <= 0:
        return
    eng.wait_ge(sem, value)


def rounds(eng, n, body):
    body(0, True, n == 1)
    if n > 2:
        with eng.Fori(1, n - 1) as it:
            body(it, False, False)
    if n > 1:
        body(n - 1, False, True)


class Chain:

    def __init__(self, eng, sem):
        self.eng, self.sem, self.per, self.lead, self.it, self.k = eng, sem, 0, 0, 0, 0

    def ahead(self):
        self.lead, self.k = self.k, 0

    def begin(self, it, first, missing=0):
        if not first and not self.per:
            self.per, self.lead = self.k + missing, self.lead - missing
        self.it, self.k = it, 0

    def step(self, ins):
        self.k += 1
        ins.then_inc(self.sem, 1)
        self.eng.wait_ge(self.sem, count(self.it, self.per, self.lead + self.k))


def seq_postln_moe_kernel(nc: bass.Bass, xT, x, w_qkv, w_proj, b_proj, router_wT, router_bias,
                          sw1, sw3, sw2, ew1, ew2, out):
    C, T = xT.shape
    N = 1024
    B = T // N
    HEADS = 16
    D = C // HEADS
    E = ew1.shape[0]
    HS = sw1.shape[1]
    SB = HS // P
    NT = N // P
    ROWS = D * PARTS + D
    SHIFT = D * PARTS
    GROUP = 4
    GROUPS = B * HEADS // GROUP
    NC = 512
    CH = N // NC
    scale = float(D) ** -0.5
    ITS = GROUPS // 2
    STEPS = 2 * CH * NT
    CHUNKS = T // NC
    CT = NC // P

    Q_PARTS = (0, 1, 2)
    K_PARTS = (2, 1, 1, 0, 0, 0)
    Q_SHIFT = D * len(Q_PARTS)
    Q_RUNS = ((0, 0, D), (D, 0, 2 * D), (3 * D, 0, Q_SHIFT))
    Q_RUNS_SHIFTED = Q_RUNS[:2] + ((3 * D, 0, Q_SHIFT + D),)
    K_RUNS = ((0, 0, SHIFT),)

    q_rows = nc.dram_tensor("q_rows", [B * HEADS, Q_SHIFT + D, N], BF16, kind="Internal").ap()
    k_rows = nc.dram_tensor("k_rows", [B * HEADS, SHIFT, N], BF16, kind="Internal").ap()

    with ExitStack() as top:
        def sb(name, shape, dt=F32, ctx=top):
            return ctx.enter_context(nc.sbuf_tensor(name, shape, dt))

        def sem(name, ctx=top):
            return ctx.enter_context(nc.semaphore(name))

        psum = top.enter_context(nc.psum_tensor("psum", [P, 8, NC], F32))
        v_all = sb("v_all", [P, GROUPS // 2, 2, NT, GROUP * D])
        attn_all = sb("attn_all", [P, GROUPS // 2, 2, CH, CT, GROUP * D])
        ident = sb("ident", [P, P])
        loose = sb("loose", [1, 1], mybir.dt.int32)
        v_w = sb("v_w", [P, 2, NT, GROUP, 32])
        q_sb = sb("q_sb", [P, 2, 2, N], BF16)
        k_sb = sb("k_sb", [P, 2, 2, N], BF16)

        x_t = sb("x_t", [P, 2, CT, C])
        a_t = sb("a_t", [P, 2, CT, C])
        tx_in = [sem(f"tx_in{i}") for i in range(2)]
        a_ready = sem("a_ready")

        wp = sb("wp", [C, C])
        rw = sb("rw", [C, E])
        s1 = sb("s1", [C, HS])
        s3 = sb("s3", [C, HS])
        s2 = sb("s2", [P, SB, C])
        e1 = sb("e1", [C, E, ew1.shape[2]])
        e2 = sb("e2", [ew1.shape[2], E, C])
        pbias = sb("pbias", [P, C])
        rbias = sb("rbias", [P, E])
        weights = (wp, rw, s1, s3, s2, e1, e2, pbias, rbias)
        weights_in = sem("weights_in")
        v_zero = sem("v_zero")

        with ExitStack() as ctx:
            w_sb = sb("w_sb", [C, 3 * C], ctx=ctx)
            x_sb = sb("x_sb", [C, 2, N], ctx=ctx)
            qk = sb("qk", [C, 2, 2, N], ctx=ctx)
            rest = sb("rest", [C, 2, N], ctx=ctx)
            parts = sb("parts", [C, 2, 2, 3, N], BF16, ctx=ctx)
            minus1 = sb("minus1", [D, 2, N], BF16, ctx=ctx)
            m_ones = sem("m_ones", ctx)
            k_ones = sem("k_ones", ctx)
            STORES = len(Q_PARTS) + len(K_PARTS) + 1
            w_in = sem("w_in", ctx)
            x_in = [sem(f"x_in{i}", ctx) for i in range(2)]
            k_abs = sb("k_abs", [C, 2], ctx=ctx)
            bound = sb("bound", [C, 2, N], BF16, ctx=ctx)
            head_of = sb("head_of", [C, HEADS], BF16, ctx=ctx)
            ones_h = sb("ones_h", [HEADS, 1], ctx=ctx)
            b_max = sb("b_max", [HEADS, B], ctx=ctx)
            b_all = sb("b_all", [HEADS, 1], ctx=ctx)
            above = sb("above", [HEADS, 1], ctx=ctx)
            k_abs_out = sem("k_abs_out", ctx)
            bound_out = sem("bound_out", ctx)
            bound_mm = sem("bound_mm", ctx)
            bound_max = sem("bound_max", ctx)
            b_step = sem("b_step", ctx)
            above_out = sem("above_out", ctx)
            above_mm = sem("above_mm", ctx)
            loose_out = sem("loose_out", ctx)
            h_one = sem("h_one", ctx)
            h_done = sem("h_done", ctx)
            qk_mm = sem("qk_mm", ctx)
            v_mm = sem("v_mm", ctx)
            qk_out = sem("qk_out", ctx)
            v_out = sem("v_out", ctx)
            hi_out = sem("hi_out", ctx)
            split = sem("split", ctx)
            rest_out = sem("rest_out", ctx)
            mid_out = sem("mid_out", ctx)
            stored = [sem(f"stored{i}", ctx) for i in range(2)]
            id_one = sem("id_one", ctx)
            id_done = sem("id_done", ctx)
            qk_ps = psum[:, 0:4, :].rearrange("p (s b) n -> p s (b n)", s=2)
            v_ps = psum[:, 4:6, :].rearrange("p b (t n) -> p (b t) n", n=P)
            b_ps = psum[:, 6:8, :].rearrange("p b n -> p (b n)")
            block = ctx.enter_context(nc.Block())

            @block.sync
            def _(sp):
                sp.dma_start(w_sb[:], w_qkv).then_inc(w_in, 16)
                sp.wait_ge(m_ones, 1)
                for hh in range(2):
                    for u in range(2):
                        sp.dma_start(k_sb[64 * hh + SHIFT:64 * hh + ROWS, u], minus1[:]).then_inc(k_ones, 16)

                def body(it, first, last):
                    for u in range(2):
                        for s, (rows, order) in enumerate(((q_rows, Q_PARTS), (k_rows, K_PARTS))):
                            sp.wait_ge(split, count(it, 4, 2 * u + s + 1))
                            for t, part in enumerate(order):
                                sp.dma_start(rows[bass.ds((it * 2 + u) * HEADS, HEADS), t * D:(t + 1) * D, :],
                                             parts[:, u, s, part]).then_inc(stored[u], 16)
                        sp.wait_ge(bound_out, count(it, 2, u + 1))
                        sp.dma_start(q_rows[bass.ds((it * 2 + u) * HEADS, HEADS), Q_SHIFT:Q_SHIFT + D, :],
                                     bound[:, u]).then_inc(stored[u], 16)
                rounds(sp, B // 2, body)
                sp.wait_ge(k_ones, 64)
                for u in range(2):
                    sp.wait_ge(stored[u], B // 2 * STORES * 16)

            @block.tensor
            def _(pe):
                pe.wait_ge(w_in, 16)

                def body(it, first, last):
                    for u in range(2):
                        pe.wait_ge(x_in[u], count(it, 16, 16))
                        for s in range(2):
                            wait(pe, qk_out, count(it, 4, 2 * u + s - 1))
                            for c in range(CH):
                                mm = pe.matmul(qk_ps[:, s, c * NC:(c + 1) * NC], w_sb[:, s * C:(s + 1) * C],
                                               x_sb[:, u, c * NC:(c + 1) * NC], start=True, stop=True)
                            mm.then_inc(qk_mm, 1)
                        wait(pe, v_out, count(it, 2, u))
                        for t in range(NT):
                            mm = pe.matmul(v_ps[:, t], x_sb[:, u, t * P:(t + 1) * P], w_sb[:, 2 * C:3 * C],
                                           start=True, stop=True)
                        mm.then_inc(v_mm, 1)
                        if not (first and u == 0):
                            bound_sums(it, u - 1)
                    if last:
                        bound_sums(it, 1)
                pe.wait_ge(h_done, 1)

                def bound_sums(it, u):
                    pe.wait_ge(bound_out, count(it, 2, u + 1))
                    wait(pe, bound_max, count(it, 2, u))
                    for c in range(CH):
                        mm = pe.matmul(b_ps[0:HEADS, c * NC:(c + 1) * NC], head_of[:],
                                       bound[:, u % 2, c * NC:(c + 1) * NC], start=True, stop=True)
                    mm.then_inc(bound_mm, 1)

                rounds(pe, B // 2, body)
                pe.wait_ge(above_out, 1)
                pe.matmul(b_ps[0:1, 0:1], ones_h[:], above[:], start=True, stop=True).then_inc(above_mm, 1)

            @block.scalar
            def _(act):
                def load_x(it, u):
                    wait(act, v_mm, count(it, 2, u - 1))
                    act.dma_start(x_sb[:, u], xT[:, bass.ds((it * 2 + u) * N, N)]).then_inc(x_in[u], 16)

                load_x(0, 0)

                def bounds(it, u):
                    v = u % 2
                    act.wait_ge(k_abs_out, count(it, 2, u + 1))
                    wait(act, stored[v], count(it + (u - v) // 2, STORES * 16, 0))
                    act.activation(bound[:, v], qk[:, v, 0], ACT.Abs, scale=k_abs[:, v:v + 1]).then_inc(bound_out, 1)

                def body(it, first, last):
                    for u in range(2):
                        if not (last and u == 1):
                            load_x(*((it, 1) if u == 0 else (it + 1, 0)))
                        for s in range(2):
                            act.wait_ge(qk_mm, count(it, 4, 2 * u + s + 1))
                            wait(act, bound_out, count(it, 2, u - 1))
                            wait(act, mid_out, count(it, 4, 2 * u + s - 3))
                            act.activation(qk[:, u, s], qk_ps[:, s], ACT.Copy,
                                           scale=scale if s == 0 else 1.0).then_inc(qk_out, 1)
                            act.wait_ge(qk_out, count(it, 4, 2 * u + s + 1))
                            if not first:
                                act.wait_ge(stored[u], count(it, STORES * 16, 0))
                            act.activation(parts[:, u, s, 0], qk[:, u, s], ACT.Copy).then_inc(hi_out, 1)
                            if s == 0 and not (first and u == 0):
                                bounds(it, u - 1)
                        act.wait_ge(v_mm, count(it, 2, u + 1))
                        for r in range(2):
                            for h in range(2):
                                ins = act.activation(v_all[:, bass.ds(4 * it + 2 * u + r, 1), h].rearrange(
                                                         "p o t c -> p (o t) c"),
                                                     v_ps[:, :, (2 * r + h) * GROUP * D:(2 * r + h + 1) * GROUP * D],
                                                     ACT.Copy)
                        ins.then_inc(v_out, 1)
                rounds(act, B // 2, body)
                bounds(B // 2 - 1, 1)

            @block.vector
            def _(dve):
                def take_rest(it, u, s):
                    dve.wait_ge(hi_out, count(it, 4, 2 * u + s + 1))
                    wait(dve, split, count(it, 4, 2 * u + s - 1))
                    dve.tensor_tensor(rest[:, s], qk[:, u, s], parts[:, u, s, 0], ALU.subtract).then_inc(rest_out, 1)

                def take_lo(it, u, s):
                    dve.wait_ge(mid_out, count(it, 4, 2 * u + s + 1))
                    dve.wait_ge(rest_out, count(it, 4, 2 * u + s + 1))
                    dve.tensor_tensor(parts[:, u, s, 2], rest[:, s], parts[:, u, s, 1],
                                      ALU.subtract).then_inc(split, 1)

                def body(it, first, last):
                    for u in range(2):
                        take_rest(it, u, 0)
                        take_rest(it, u, 1)
                        take_lo(it, u, 0)
                        dve.tensor_reduce(k_abs[:, u:u + 1], qk[:, u, 1], AX.X, ALU.max,
                                          apply_absolute_value=True).then_inc(k_abs_out, 1)
                        take_lo(it, u, 1)
                        if not (first and u == 0):
                            largest(it, u - 1)
                    if last:
                        largest(it, 1)

                def largest(it, u):
                    dve.wait_ge(bound_mm, count(it, 2, u + 1))
                    dve.tensor_reduce(b_max[:, bass.ds(it * 2 + u, 1)], b_ps[0:HEADS], AX.X,
                                      ALU.max).then_inc(bound_max, 1)

                rounds(dve, B // 2, body)
                dve.wait_ge(bound_max, B)
                dve.tensor_reduce(b_all[:], b_max[:], AX.X, ALU.max).then_inc(b_step, 1)
                dve.wait_ge(b_step, 1)
                dve.tensor_scalar(above[:], b_all[:], SAFE, None, ALU.is_gt).then_inc(above_out, 1)
                dve.wait_ge(above_mm, 1)
                dve.tensor_copy(loose[:], b_ps[0:1, 0:1]).then_inc(loose_out, 1)

            @block.gpsimd
            def _(pool):
                pool.memset(ident[:], 1.0).then_inc(id_one, 1)
                pool.wait_ge(id_one, 1)
                pool.affine_select(out=ident[:], in_=ident[:], compare_op=ALU.is_equal, fill=0.0, base=0,
                                   pattern=[[-1, P]], channel_multiplier=1).then_inc(id_done, 1)

                pool.memset(minus1[:], -1.0).then_inc(m_ones, 1)
                pool.memset(ones_h[:], 1.0).then_inc(h_one, 1)
                pool.memset(head_of[:], 1.0).then_inc(h_one, 1)
                pool.wait_ge(h_one, 2)
                pool.affine_select(out=head_of[:], in_=head_of[:], compare_op=ALU.is_ge, fill=0.0, base=0,
                                   pattern=[[-D, HEADS]], channel_multiplier=1).then_inc(h_one, 1)
                pool.wait_ge(h_one, 3)
                pool.affine_select(out=head_of[:], in_=head_of[:], compare_op=ALU.is_gt, fill=0.0, base=D,
                                   pattern=[[D, HEADS]], channel_multiplier=-1).then_inc(h_done, 1)
                pool.memset(v_w[:], 0.0).then_inc(v_zero, 1)
                pool.wait_ge(v_zero, 1)
                pool.memset(v_w[:, :, :, :, D:D + 1], 1.0).then_inc(v_zero, 1)

                def body(it, first, last):
                    for u in range(2):
                        for s in range(2):
                            pool.wait_ge(hi_out, count(it, 4, 2 * u + s + 1))
                            pool.tensor_tensor(parts[:, u, s, 1], qk[:, u, s], parts[:, u, s, 0],
                                               ALU.subtract).then_inc(mid_out, 1)
                rounds(pool, B // 2, body)

        LOADED = 2 * (len(Q_RUNS) + len(K_RUNS)) * 16

        def load_rows(eng, rows, runs, dst, u, it, done):
            for hh in range(2):
                for to, start, n in runs:
                    eng.dma_start(dst[64 * hh + to:64 * hh + to + n, u],
                                  rows[bass.ds((it * 2 + u) * GROUP, GROUP), start:start + n, :].rearrange(
                                      "(pair hh) r n -> hh r pair n", hh=2)[hh]).then_inc(done, 16)

        with ExitStack() as ctx:
            mx = sb("mx", [P, 2, NT, GROUP], ctx=ctx)
            mxT = sb("mxT", [GROUP, 2, N], ctx=ctx)
            shift = sb("shift", [GROUP, D, N], BF16, ctx=ctx)
            qk_in = [sem(f"mqk_in{i}", ctx) for i in range(2)]
            s_mm = sem("ms_mm", ctx)
            s_max = sem("ms_max", ctx)
            m_tr = sem("m_tr", ctx)
            m_split = sem("m_split", ctx)
            m_zero = sem("m_zero", ctx)
            m_step = sem("m_step", ctx)
            m_store = sem("m_store", ctx)
            TILES = GROUP * NT
            s_ps = psum[:, 0:4, :].rearrange("p (s b) n -> p s (b n)", s=2)
            t_ps = psum[:, 4:6, :].rearrange("p b n -> p (b n)")
            block = ctx.enter_context(nc.Block())

            @block.sync
            def _(sp):
                def body(it, first, last):
                    for u in range(2):
                        wait(sp, s_mm, count(it, 2 * TILES, (u - 1) * TILES))
                        load_rows(sp, q_rows, Q_RUNS, q_sb, u, it, qk_in[u])
                        load_rows(sp, k_rows, K_RUNS, k_sb, u, it, qk_in[u])
                with sp.If(sp.value_load(loose[:], min_val=0, max_val=HEADS) > 0):
                    rounds(sp, ITS, body)

            @block.tensor
            def _(pe):
                def body(it, first, last):
                    for u in range(2):
                        pe.wait_ge(qk_in[u], count(it, LOADED, LOADED))
                        for i in range(TILES):
                            j, t = divmod(i, NT)
                            pair, hh = divmod(j, 2)
                            rows = slice(64 * hh, 64 * hh + SHIFT)
                            wait(pe, s_max, count(it, 2 * TILES, u * TILES + i - 1))
                            for c in range(CH):
                                mm = pe.matmul(s_ps[:, i % 2, c * NC:(c + 1) * NC],
                                               q_sb[rows, u, pair, t * P:(t + 1) * P],
                                               k_sb[rows, u, pair, c * NC:(c + 1) * NC], start=True, stop=True)
                            mm.then_inc(s_mm, 1)
                        pe.wait_ge(s_max, count(it, 2 * TILES, (u + 1) * TILES))
                        wait(pe, m_split, count(it, 2, u))
                        for t in range(NT):
                            mm = pe.transpose(t_ps[0:GROUP, t * P:(t + 1) * P], mx[:, u, t, :], ident[:])
                        mm.then_inc(m_tr, 1)
                with pe.If(pe.value_load(loose[:], min_val=0, max_val=HEADS) > 0):
                    rounds(pe, ITS, body)

            @block.vector
            def _(dve):
                chain = Chain(dve, m_step)

                def body(it, first, last):
                    chain.begin(it, first)
                    for u in range(2):
                        for i in range(TILES):
                            j, t = divmod(i, NT)
                            dve.wait_ge(s_mm, count(it, 2 * TILES, u * TILES + i + 1))
                            dve.tensor_reduce(mx[:, u, t, j:j + 1], s_ps[:, i % 2], AX.X,
                                              ALU.max).then_inc(s_max, 1)
                        dve.wait_ge(m_tr, count(it, 2, u + 1))
                        wait(dve, m_store, count(it, 32, 16 * u))
                        chain.step(dve.tensor_copy(shift[:, 0], t_ps[0:GROUP]))
                        chain.step(dve.tensor_tensor(mxT[:, 0], t_ps[0:GROUP], shift[:, 0], ALU.subtract))
                        chain.step(dve.tensor_copy(shift[:, 1], mxT[:, 0]))
                        chain.step(dve.tensor_tensor(mxT[:, 1], mxT[:, 0], shift[:, 1], ALU.subtract))
                        dve.tensor_copy(shift[:, 2], mxT[:, 1]).then_inc(m_split, 1)
                with dve.If(dve.value_load(loose[:], min_val=0, max_val=HEADS) > 0):
                    dve.memset(shift[:], 0.0).then_inc(m_zero, 1)
                    dve.wait_ge(m_zero, 1)
                    rounds(dve, ITS, body)

            @block.gpsimd
            def _(pool):
                def body(it, first, last):
                    for u in range(2):
                        pool.wait_ge(m_split, count(it, 2, u + 1))
                        pool.dma_start(q_rows[bass.ds((it * 2 + u) * GROUP, GROUP), Q_SHIFT:Q_SHIFT + D, :],
                                       shift[:]).then_inc(m_store, 16)
                with pool.If(pool.value_load(loose[:], min_val=0, max_val=HEADS) > 0):
                    rounds(pool, ITS, body)
                    pool.wait_ge(m_store, GROUPS * 16)

        with ExitStack() as ctx:
            p_sb = sb("p_sb", [P, EXP_SLOTS, GROUP, NC], ctx=ctx)
            o_sb = sb("o_sb", [P, 2, NC], ctx=ctx)
            r_sb = sb("r_sb", [P, CT, GROUP], ctx=ctx)
            rows_in = [sem(f"rows_in{i}", ctx) for i in range(2)]
            v_ready = sem("v_ready", ctx)
            scores = sem("scores", ctx)
            exps = sem("exps", ctx)
            pv = sem("pv", ctx)
            o_mm = sem("o_mm", ctx)
            o_out = sem("o_out", ctx)
            o_tr = sem("o_tr", ctx)
            recip = sem("recip", ctx)
            o_norm = sem("o_norm", ctx)
            block = ctx.enter_context(nc.Block())
            PAIRS = 2 * STEPS
            OCH = 2 * CH

            def slot(p):
                q = p % PAIRS
                return 1 if q == PAIRS - 1 else q % PAIRS_IN_FLIGHT

            def last_user(p):
                return max(r for r in range(p - 2 * PAIRS_IN_FLIGHT, p) if slot(r) == slot(p))

            @block.sync
            def _(sp):
                def body(it, first, last):
                    for u in range(2):
                        wait(sp, scores, count(it, PAIRS, (u + 1) * PAIRS // 2 - PAIRS))
                        load_rows(sp, q_rows, Q_RUNS_SHIFTED, q_sb, u, it, rows_in[u])
                        load_rows(sp, k_rows, K_RUNS, k_sb, u, it, rows_in[u])
                    if first:
                        for dst, src in zip(weights, (
                                w_proj, router_wT, sw1, sw3, sw2.rearrange("(s h) c -> h s c", h=P),
                                ew1.rearrange("e c h -> c e h"), ew2.rearrange("e h c -> h e c"),
                                b_proj, router_bias)):
                            sp.dma_start(dst[:], src).then_inc(weights_in, 16)
                        sp.dma_start(x_t[:, 0], x[0:NC, :].rearrange("(t p) c -> p t c", p=P)).then_inc(tx_in[0], 16)
                rounds(sp, ITS, body)

            @block.gpsimd
            def _(pool):
                def body(it, first, last):
                    for u in range(2):
                        wait(pool, pv, count(it, STEPS, (u + 1) * STEPS // 2 - STEPS))
                        src = v_all[:, bass.ds(it, 1), u].rearrange("p o t (j d) -> p (o t) j d", j=GROUP)
                        pool.tensor_copy(v_w[:, u, :, :, 0:D], src).then_inc(v_ready, 1)
                rounds(pool, ITS, body)
                pool.wait_ge(o_norm, 2 * OCH)
                for g in range(HEADS // GROUP):
                    ins = pool.tensor_copy(a_t[:, 0, :, g * GROUP * D:(g + 1) * GROUP * D],
                                           attn_all[:, g // 2, g % 2, 0])
                ins.then_inc(a_ready, 1)

            @block.tensor
            def _(pe):
                for _ in range(WARM_UP):
                    pe.matmul(psum[:, 7], ident[:], v_all[:, 0].rearrange("p g t c -> p (g t c)"),
                              start=True, stop=True)
                pe.wait_ge(v_zero, 2)

                def score_pair(it, p):
                    nxt, q = divmod(p, PAIRS)
                    u, q = divmod(q, CH * NT * 2)
                    c, q = divmod(q, NT * 2)
                    t, pair = divmod(q, 2)
                    if c == 0 and t == 0 and pair == 0:
                        pe.wait_ge(rows_in[u], count(it + nxt, LOADED, LOADED))
                    wait(pe, exps, count(it, PAIRS, last_user(p) + 1))
                    for hh in range(2):
                        rows = slice(64 * hh, 64 * hh + ROWS)
                        mm = pe.matmul(psum[:, 2 * slot(p) + hh], k_sb[rows, u, pair, t * P:(t + 1) * P],
                                       q_sb[rows, u, pair, c * NC:(c + 1) * NC], start=True, stop=True)
                    mm.then_inc(scores, 1)

                def weigh(it, s):
                    o, t = divmod(s, NT)
                    u = o // CH
                    if o % CH == 0 and t == 0:
                        pe.wait_ge(v_ready, count(it, 2, u + 1))
                    if t == 0:
                        wait(pe, o_norm, count(it, OCH, o - 1))
                    pe.wait_ge(exps, count(it, PAIRS, 2 * s + 2))
                    for j in range(GROUP):
                        mm = pe.matmul(psum[32 * j:32 * j + 32, 6 + o % 2], v_w[:, u, t, j, :],
                                       p_sb[:, s % EXP_SLOTS, j, :], start=(t == 0), stop=(t == NT - 1))
                    mm.then_inc(pv, 1)

                def turn(it, o):
                    pe.wait_ge(o_out, count(it, OCH, o + 1))
                    for t in range(CT):
                        mm = pe.transpose(psum[:, 6 + o % 2, t * P:(t + 1) * P], o_sb[:, o % 2, t * P:(t + 1) * P],
                                          ident[:])
                    mm.then_inc(o_tr, 1)

                for p in range(PAIRS_IN_FLIGHT):
                    score_pair(0, p)

                def body(it, first, last):
                    for s in range(STEPS):
                        for p in (2 * s + PAIRS_IN_FLIGHT, 2 * s + PAIRS_IN_FLIGHT + 1):
                            if not (last and p >= PAIRS):
                                score_pair(it, p)
                        weigh(it, s)
                        if s % NT == 1 and not (first and s < NT):
                            turn(it, s // NT - 1)
                    if last:
                        turn(it, OCH - 1)
                rounds(pe, ITS, body)

            @block.scalar
            def _(act):
                def body(it, first, last):
                    for p in range(PAIRS):
                        s, pair = divmod(p, 2)
                        act.wait_ge(scores, count(it, PAIRS, p + 1))
                        if pair == 0:
                            wait(act, pv, count(it, STEPS, s - EXP_SLOTS + 1))
                        act.activation(p_sb[:, s % EXP_SLOTS, 2 * pair:2 * pair + 2, :],
                                       psum[:, 2 * slot(p):2 * slot(p) + 2, :], ACT.Exp).then_inc(exps, 1)
                rounds(act, ITS, body)

            @block.vector
            def _(dve):
                def body(it, first, last):
                    for o in range(OCH):
                        dve.wait_ge(pv, count(it, STEPS, NT * (o + 1)))
                        dve.tensor_copy(o_sb[:, o % 2], psum[:, 6 + o % 2]).then_inc(o_out, 1)
                        dve.wait_ge(o_tr, count(it, OCH, o + 1))
                        turned = psum[:, 6 + o % 2, :].rearrange("p (t j r) -> p t j r", t=CT, j=GROUP)
                        dve.reciprocal(r_sb[:], turned[:, :, :, D]).then_inc(recip, 1)
                        dve.wait_ge(recip, count(it, OCH, o + 1))
                        dst = attn_all[:, bass.ds(it, 1), o // CH, o % CH].rearrange(
                            "p o t (j d) -> p (o t) j d", j=GROUP)
                        dve.tensor_tensor(dst, turned[:, :, :, 0:D],
                                          r_sb[:].unsqueeze(3).broadcast_to([P, CT, GROUP, D]),
                                          ALU.mult).then_inc(o_norm, 1)
                rounds(dve, ITS, body)

        mixed_tail(nc, psum, attn_all, ident, x_t, a_t, tx_in, a_ready, x, weights, weights_in, E, ew1.shape[2], SB, out)


def mixed_tail(nc, psum, attn_all, ident, x_t, a_t, x_in, a_ready, x, weights, weights_in, E, H, SB, out):
    T, C = x.shape
    NC = 512
    CT = NC // P
    CHUNKS = T // NC
    CH = 2
    QUARTERS = attn_all.shape[1] * 2 * CH // CHUNKS
    UPS = 2 * SB + E
    DOWNS = 1 + E
    LAG = 2 * SB + 1
    H_BANKS = (2, 3, 4)
    Y_BANKS = (5, 6, 7)

    with ExitStack() as ctx:
        def sb(name, shape, dt=F32):
            return ctx.enter_context(nc.sbuf_tensor(name, shape, dt))

        def sem(name):
            return ctx.enter_context(nc.semaphore(name))

        before = sb("before", [P, E, E])
        aT = sb("aT", [C, NC])
        u1 = sb("u1", [P, CT, C])
        x1 = sb("x1", [P, 2, CT, C])
        x1T = sb("x1T", [C, 2, NC])
        st_2 = sb("st_2", [P, 2, CT, 6])
        mean_2 = sb("mean_2", [P, 2, CT])
        apart_2 = sb("apart_2", [P, 2, CT])
        ve_2 = sb("ve_2", [P, 2, CT])
        rstd_2 = sb("rstd_2", [P, 2, CT])
        neg_half = sb("neg_half", [P, CT])
        sg = sb("sg", [P, 2, CT, E])
        sel = sb("sel", [P, CT, E])
        gt = sb("gt", [P, CT, E, E])
        eq = sb("eq", [P, CT, E, E])
        rank = sb("rank", [P, CT, E])
        mask = sb("mask", [P, CT, E])
        sm = sb("sm", [P, CT, E])
        hm = sb("hm", [P, CT, E])
        den = sb("den", [P, CT])
        den1 = sb("den1", [P, CT])
        okd = sb("okd", [P, CT])
        rden = sb("rden", [P, CT])
        half = sb("half", [P, CT])
        comb = sb("comb", [P, CT, E])
        sig = sb("sig", [P, 2, NC])
        silu = sb("silu", [P, 2, NC])
        gated = sb("gated", [P, SB, NC])
        act_h = sb("act_h", [H, 3, NC])
        acc = sb("acc", [P, 2, CT, C])
        o_t = sb("o_t", [P, 2, CT, C])

        consts = sem("consts")
        x_biased = sem("x_biased")
        a_tr = sem("a_tr")
        a_out = sem("a_out")
        proj = sem("proj")
        u_ready = sem("u_ready")
        var_in = [sem(f"var_in{i}") for i in range(2)]
        std_out = [sem(f"std_out{i}") for i in range(2)]
        x1_ready = sem("x1_ready")
        x1_tr = sem("x1_tr")
        x1T_out = sem("x1T_out")
        logits = sem("logits")
        sig_out = sem("sig_out")
        comb_out = sem("comb_out")
        up = sem("up")
        sig_h = sem("sig_h")
        silu_out = sem("silu_out")
        gated_out = sem("gated_out")
        gelu_out = sem("gelu_out")
        down = sem("down")
        added = sem("added")
        dve_step = sem("t_step")
        pool_step = sem("p_step")
        normed = sem("normed")
        stored = [sem(f"t_stored{i}") for i in range(2)]
        WEIGHTS = len(weights)
        wp, rw, s1, s3, s2, e1, e2, pbias, rbias = weights

        block = ctx.enter_context(nc.Block())
        ROUNDS = CHUNKS // CH

        def banks(i):
            return psum[:, i].rearrange("p (t c) -> p t c", t=CT)

        @block.sync
        def _(sp):
            def load_x(it, u):
                wait(sp, u_ready, count(it, CH, u - 1))
                sp.dma_start(x_t[:, u], x[bass.ds((it * CH + u) * NC, NC), :].rearrange(
                    "(t p) c -> p t c", p=P)).then_inc(x_in[u], 16)


            def body(it, first, last):
                for u in range(CH):
                    if not (last and u == CH - 1):
                        load_x(*((it, u + 1) if u + 1 < CH else (it + 1, 0)))
                    if not (first and u == 0):
                        v = (u - 1) % CH
                        done = it * CH + u - 1
                        sp.wait_ge(normed, count(it, CH, u))
                        sp.dma_start(out[bass.ds(done * NC, NC), :].rearrange("(t p) c -> p t c", p=P),
                                     o_t[:, v]).then_inc(stored[v], 16)
            rounds(sp, ROUNDS, body)
            sp.wait_ge(normed, CHUNKS)
            sp.dma_start(out[(CHUNKS - 1) * NC:, :].rearrange("(t p) c -> p t c", p=P),
                         o_t[:, CH - 1]).then_inc(stored[CH - 1], 16)
            for v in range(CH):
                sp.wait_ge(stored[v], ROUNDS * 16)

        @block.gpsimd
        def _(pool):
            pool.memset(neg_half[:], -0.5).then_inc(consts, 1)
            pool.memset(before[:], 1.0).then_inc(consts, 1)
            pool.wait_ge(consts, 2)
            pool.affine_select(out=before[:], in_=before[:], compare_op=ALU.is_gt, fill=0.0, base=0,
                               pattern=[[1, E], [-1, E]], channel_multiplier=0).then_inc(consts, 1)
            pool.wait_ge(weights_in, 16 * WEIGHTS)
            pool.wait_ge(consts, 3)

            def front(it, u):
                if not (isinstance(it, int) and it == 0 and u == 0):
                    wait(pool, a_tr, count(it, CH, u - 1))
                    for g in range(QUARTERS):
                        src = attn_all[:, bass.ds(it * 2 + g // 2, 1), g % 2, u].rearrange("p o t c -> p (o t) c")
                        ins = pool.tensor_copy(a_t[:, u, :, g * (C // QUARTERS):(g + 1) * (C // QUARTERS)], src)
                    ins.then_inc(a_ready, 1)
                pool.wait_ge(x_in[u], count(it, 16, 16))
                pool.tensor_tensor(x_t[:, u], x_t[:, u], pbias[:].unsqueeze(1).broadcast_to([P, CT, C]),
                                   ALU.add).then_inc(x_biased, 1)

            def power(it, u, which):
                pool.wait_ge(var_in[which], count(it, CH, u + 1))
                pool.tensor_tensor(rstd_2[:, which], ve_2[:, which], neg_half[:], ALU.pow).then_inc(std_out[which], 1)

            front(0, 0)
            power(0, 0, 0)

            def body(it, first, last):
                for u in range(CH):
                    ahead = (it, u + 1) if u + 1 < CH else (it + 1, 0)
                    more = not (last and u == CH - 1)
                    if more:
                        front(*ahead)
                    if more:
                        power(*ahead, 0)
                    if not (first and u == 0):
                        power(it, u - 1, 1)
            rounds(pool, ROUNDS, body)
            power(ROUNDS - 1, CH - 1, 1)

        @block.tensor
        def _(pe):
            pe.wait_ge(weights_in, 16 * WEIGHTS)

            def front_attn(it, u):
                pe.wait_ge(a_ready, count(it, CH, u + 1))
                wait(pe, x1T_out, count(it, CH, u))
                for t in range(CT):
                    mm = pe.transpose(psum[:, 0, t * P:(t + 1) * P], a_t[:, u, t, :], ident[:])
                mm.then_inc(a_tr, 1)

            def front_proj(it, u):
                pe.wait_ge(a_out, count(it, CH, u + 1))
                wait(pe, sig_out, count(it, CH, u))
                for t in range(CT):
                    mm = pe.matmul(psum[:, 1, t * P:(t + 1) * P], aT[:, t * P:(t + 1) * P], wp[:],
                                   start=True, stop=True)
                mm.then_inc(proj, 1)

            def front_turn(it, u):
                pe.wait_ge(x1_ready, count(it, CH, u + 1))
                for t in range(CT):
                    mm = pe.transpose(psum[:, 0, t * P:(t + 1) * P], x1[:, u, t, :], ident[:])
                mm.then_inc(x1_tr, 1)

            def front_router(it, u):
                pe.wait_ge(x1T_out, count(it, CH, u + 1))
                for t in range(CT):
                    mm = pe.matmul(psum[:, 1, t * E:(t + 1) * E], x1T[:, u, t * P:(t + 1) * P], rw[:],
                                   start=True, stop=True)
                mm.then_inc(logits, 1)

            def rise(it, u, n, weights):
                wait(pe, *up_free(it, u, n - 3))
                pe.matmul(psum[:, H_BANKS[n % 3]], weights, x1T[:, u], start=True, stop=True).then_inc(up, 1)

            def up_free(it, u, n):
                if n < 0:
                    u, n = u - 1, n + UPS
                if n < 2 * SB:
                    return gated_out if n % 2 else silu_out, count(it, CH * SB, SB * u + n // 2 + 1)
                return gelu_out, count(it, CH * E, E * u + n - 2 * SB + 1)

            def fall(it, u, n):
                wait(pe, added, count(it, CH * DOWNS, DOWNS * u + n - 2))
                if n == 0:
                    pe.wait_ge(gated_out, count(it, CH * SB, SB * (u + 1)))
                else:
                    pe.wait_ge(gelu_out, count(it, CH * E, E * u + n))
                y = banks(Y_BANKS[n % 3])
                for t in range(CT):
                    tok = slice(t * P, (t + 1) * P)
                    if n:
                        mm = pe.matmul(y[:, t], act_h[:, (n - 1) % 3, tok], e2[:, n - 1], start=True, stop=True)
                    else:
                        for s in range(SB):
                            mm = pe.matmul(y[:, t], gated[:, s, tok], s2[:, s], start=(s == 0), stop=(s == SB - 1))
                mm.then_inc(down, 1)

            front_attn(0, 0)
            front_proj(0, 0)
            for _ in range(TAIL_WARM_UP):
                pe.matmul(psum[:, H_BANKS[0]], ident[:], attn_all[:, 0].rearrange("p g c t d -> p (g c t d)")[:, 0:NC],
                          start=True, stop=True)
            front_turn(0, 0)
            front_router(0, 0)

            def body(it, first, last):
                for u in range(CH):
                    ahead = (it, u + 1) if u + 1 < CH else (it + 1, 0)
                    front = [] if last and u == CH - 1 else [front_attn, front_proj, front_turn, front_router]

                    def next_front():
                        if front:
                            front.pop(0)(*ahead)

                    for n in range(UPS):
                        if n < 2 * SB:
                            rise(it, u, n, (s3 if n % 2 else s1)[:, n // 2 * P:(n // 2 + 1) * P])
                        else:
                            rise(it, u, n, e1[:, n - 2 * SB])
                        if n in (1, 2 * SB - 1, UPS - 4, UPS - 2):
                            next_front()
                        if n >= LAG:
                            fall(it, u, n - LAG)
                        elif n < DOWNS + LAG - UPS and not (first and u == 0):
                            fall(it, u - 1, n + UPS - LAG)
                if last:
                    for n in range(UPS - LAG, DOWNS):
                        fall(it, CH - 1, n)
            rounds(pe, ROUNDS, body)

        @block.scalar
        def _(act):
            def take_attn(it, u):
                act.wait_ge(a_tr, count(it, CH, u + 1))
                wait(act, proj, count(it, CH, u))
                act.activation(aT[:], psum[:, 0], ACT.Copy).then_inc(a_out, 1)

            def take_x1T(it, u):
                act.wait_ge(x1_tr, count(it, CH, u + 1))
                wait(act, up, count(it, CH * UPS, UPS * (u - 1)))
                act.activation(x1T[:, u], psum[:, 0], ACT.Copy).then_inc(x1T_out, 1)

            def route(it, u):
                act.wait_ge(logits, count(it, CH, u + 1))
                wait(act, comb_out, count(it, CH, u - 1))
                act.activation(sg[:, u], psum[:, 1, 0:CT * E].rearrange("p (t e) -> p t e", e=E),
                               ACT.Sigmoid).then_inc(sig_out, 1)

            take_attn(0, 0)
            take_x1T(0, 0)

            def body(it, first, last):
                for u in range(CH):
                    ahead = (it, u + 1) if u + 1 < CH else (it + 1, 0)
                    more = not (last and u == CH - 1)
                    route(it, u)
                    for s in range(SB):
                        act.wait_ge(up, count(it, CH * UPS, UPS * u + 2 * s + 1))
                        wait(act, silu_out, count(it, CH * SB, SB * u + s - 1))
                        act.activation(sig[:, s % 2], psum[:, H_BANKS[2 * s % 3]], ACT.Sigmoid).then_inc(sig_h, 1)
                        if s == 0 and more:
                            take_attn(*ahead)
                    for e in range(E):
                        if e == E // 2 + 1 and more:
                            take_x1T(*ahead)
                        act.wait_ge(up, count(it, CH * UPS, UPS * u + 2 * SB + e + 1))
                        user = e - 3 if e >= 3 else max(range(e, E, 3)) - E - 1
                        wait(act, down, count(it, CH * DOWNS, DOWNS * u + user + 2))
                        act.activation(act_h[:, e % 3], psum[:, H_BANKS[(2 * SB + e) % 3]],
                                       ACT.Gelu).then_inc(gelu_out, 1)
            rounds(act, ROUNDS, body)

        @block.vector
        def _(dve):
            dve.wait_ge(weights_in, 16 * WEIGHTS)
            dve.wait_ge(consts, 3)
            chain = Chain(dve, dve_step)
            NORM_STEPS = 3

            def statistics(which, src):
                st, mean, apart, ve = (x[:, which] for x in (st_2, mean_2, apart_2, ve_2))
                for t in range(CT):
                    ins = dve.bn_stats(st[:, t], src[:, t])
                chain.step(ins)
                (mean_e, var_e), (mean_o, var_o) = ((st[:, :, 3 * i + 1], st[:, :, 3 * i + 2]) for i in range(2))
                dve.tensor_tensor(mean, mean_e, mean_o, ALU.add)
                dve.tensor_tensor(apart, mean_e, mean_o, ALU.subtract)
                chain.step(dve.tensor_tensor(ve, var_e, var_o, ALU.add))
                dve.tensor_scalar(mean, mean, 0.5, None, ALU.mult)
                dve.tensor_scalar(ve, ve, 1.0 / C, LN_EPS, ALU.mult, ALU.add)
                chain.step(dve.scalar_tensor_tensor(out=apart, in0=apart, scalar=0.25, in1=apart,
                                                    op0=ALU.mult, op1=ALU.mult))
                dve.tensor_tensor(ve, ve, apart, ALU.add).then_inc(var_in[which], 1)

            def normalise(it, u, which, src, dst, done):
                dve.wait_ge(std_out[which], count(it, CH, u + 1))
                for t in range(CT):
                    ins = dve.tensor_scalar(dst[:, t], src[:, t], mean_2[:, which, t:t + 1],
                                            rstd_2[:, which, t:t + 1], ALU.subtract, ALU.mult)
                ins.then_inc(done, 1)

            def first_sum(it, u):
                dve.wait_ge(proj, count(it, CH, u + 1))
                dve.wait_ge(x_biased, count(it, CH, u + 1))
                dve.tensor_tensor(u1[:], banks(1), x_t[:, u], ALU.add).then_inc(u_ready, 1)
                dve.wait_ge(u_ready, count(it, CH, u + 1))
                statistics(0, u1)

            def first_norm(it, u):
                normalise(it, u, 0, u1, x1[:, u], x1_ready)

            def last_norm(it, u):
                v = u % CH
                wait(dve, stored[v], count(it + (u - v) // CH, 16, 0))
                normalise(it, u, 1, acc[:, v], o_t[:, v], normed)

            def gates(it, u):
                s = sg[:, u]
                dve.wait_ge(sig_out, count(it, CH, u + 1))
                chain.step(dve.tensor_tensor(sel[:], s, rbias[:].unsqueeze(1).broadcast_to([P, CT, E]), ALU.add))
                one = sel[:].unsqueeze(3).broadcast_to([P, CT, E, E])
                other = sel[:].unsqueeze(2).broadcast_to([P, CT, E, E])
                dve.tensor_tensor(gt[:], other, one, ALU.is_gt)
                chain.step(dve.tensor_tensor(eq[:], other, one, ALU.is_equal))
                chain.step(dve.tensor_tensor(eq[:], eq[:], before[:].unsqueeze(1).broadcast_to([P, CT, E, E]),
                                             ALU.mult))
                chain.step(dve.tensor_tensor(gt[:], gt[:], eq[:], ALU.add))
                chain.step(dve.tensor_reduce(rank[:], gt[:], AX.X, ALU.add))
                chain.step(dve.scalar_tensor_tensor(out=sm[:], in0=rank[:], scalar=1.5, in1=s,
                                                    op0=ALU.is_lt, op1=ALU.mult))
                chain.step(dve.tensor_reduce(den[:], sm[:], AX.X, ALU.add))
                dve.tensor_scalar(mask[:], rank[:], 1.5, None, ALU.is_lt)
                dve.tensor_scalar(okd[:], den[:], 1e-9, None, ALU.is_gt)
                chain.step(dve.tensor_scalar(den1[:], den[:], 1e-9, None, ALU.add))
                dve.tensor_scalar(half[:], okd[:], -0.5, 0.5, ALU.mult, ALU.add)
                chain.step(dve.reciprocal(rden[:], den1[:]))
                dve.tensor_tensor(hm[:], mask[:], half[:].unsqueeze(2).broadcast_to([P, CT, E]), ALU.mult)
                chain.step(dve.tensor_tensor(rden[:], rden[:], okd[:], ALU.mult))
                chain.step(dve.tensor_tensor(sm[:], sm[:], rden[:].unsqueeze(2).broadcast_to([P, CT, E]), ALU.mult))
                dve.tensor_tensor(comb[:], sm[:], hm[:], ALU.add).then_inc(comb_out, 1)
                dve.wait_ge(comb_out, count(it, CH, u + 1))

            def add_expert(it, u, n):
                dve.wait_ge(down, count(it, CH * DOWNS, DOWNS * u + n + 1))
                y, v = banks(Y_BANKS[n % 3]), u % CH
                if n == 0:
                    dve.tensor_tensor(acc[:, v], y, x1[:, v], ALU.add).then_inc(added, 1)
                else:
                    for t in range(CT):
                        ins = dve.scalar_tensor_tensor(out=acc[:, v, t], in0=y[:, t], scalar=comb[:, t, n - 1:n],
                                                       in1=acc[:, v, t], op0=ALU.mult, op1=ALU.add)
                    ins.then_inc(added, 1)
                dve.wait_ge(added, count(it, CH * DOWNS, DOWNS * u + n + 1))

            first_sum(0, 0)
            first_norm(0, 0)
            chain.ahead()

            def body(it, first, last):
                chain.begin(it, first, NORM_STEPS)
                for u in range(CH):
                    ahead = (it, u + 1) if u + 1 < CH else (it + 1, 0)
                    more = not (last and u == CH - 1)
                    begun = not (first and u == 0)
                    late = list(range(UPS - LAG, DOWNS)) if begun else []
                    for s in range(SB):
                        if late:
                            add_expert(it, u - 1, late.pop(0))
                        dve.wait_ge(sig_h, count(it, CH * SB, SB * u + s + 1))
                        dve.tensor_tensor(silu[:, s % 2], psum[:, H_BANKS[2 * s % 3]], sig[:, s % 2],
                                          ALU.mult).then_inc(silu_out, 1)
                        dve.wait_ge(silu_out, count(it, CH * SB, SB * u + s + 1))
                        dve.wait_ge(up, count(it, CH * UPS, UPS * u + 2 * s + 2))
                        wait(dve, down, count(it, CH * DOWNS, DOWNS * (u - 1) + 1))
                        dve.tensor_tensor(gated[:, s], psum[:, H_BANKS[(2 * s + 1) % 3]], silu[:, s % 2],
                                          ALU.mult).then_inc(gated_out, 1)
                    assert not late
                    if more:
                        first_sum(*ahead)
                    gates(it, u)
                    if more:
                        first_norm(*ahead)
                    add_expert(it, u, 0)
                    for n in range(1, UPS - LAG):
                        add_expert(it, u, n)
                        if n == 2 and begun:
                            statistics(1, acc[:, (u - 1) % CH])
                        if n == 3 and begun:
                            last_norm(it, u - 1)
                if last:
                    for n in range(UPS - LAG, DOWNS):
                        add_expert(it, CH - 1, n)
                    statistics(1, acc[:, CH - 1])
                    last_norm(it, CH - 1)
            rounds(dve, ROUNDS, body)


def kernel(L0_attn_x, L0_attn_w_qkv, L0_attn_w_proj, L0_attn_b_proj, L0_ffn_router_w, L0_ffn_router_bias,
           L0_ffn_sw1, L0_ffn_sw3, L0_ffn_sw2, L0_ffn_ew1, L0_ffn_ew2):
    import numpy as np
    import concourse.bacc as bacc
    from concourse.bass_utils import run_bass_kernel_spmd

    x = np.asarray(L0_attn_x)
    b, n, c = x.shape
    x = np.ascontiguousarray(x.reshape(b * n, c))
    rows = np.zeros((P, 1), np.float32).shape[0]
    arrays = {
        "xT": np.ascontiguousarray(x.T), "x": x, "w_qkv": np.asarray(L0_attn_w_qkv),
        "w_proj": np.asarray(L0_attn_w_proj),
        "b_proj": np.ascontiguousarray(np.broadcast_to(np.asarray(L0_attn_b_proj), (rows, c))),
        "router_wT": np.ascontiguousarray(np.asarray(L0_ffn_router_w).T),
        "router_bias": np.ascontiguousarray(
            np.broadcast_to(np.asarray(L0_ffn_router_bias), (rows, L0_ffn_router_bias.shape[0]))),
        "sw1": np.asarray(L0_ffn_sw1), "sw3": np.asarray(L0_ffn_sw3), "sw2": np.asarray(L0_ffn_sw2),
        "ew1": np.asarray(L0_ffn_ew1), "ew2": np.asarray(L0_ffn_ew2),
    }
    nc = bacc.Bacc("TRN2", target_bir_lowering=False, num_devices=1)
    args = [nc.dram_tensor(f"in_{k}", a.shape, mybir.dt.from_np(a.dtype), kind="ExternalInput").ap()
            for k, a in arrays.items()]
    out = nc.dram_tensor("result", x.shape, F32, kind="ExternalOutput").ap()
    seq_postln_moe_kernel(nc, *args, out)
    r = run_bass_kernel_spmd(nc, [{f"in_{k}": a for k, a in arrays.items()}], core_ids=[0])
    return r.results[0]["result"].reshape(b, n, c)
```
